# Optimizing a Trainium2 kernel written in Bass

```python
import numpy as np
import jax
import jax.numpy as jnp

def _softmax(x, axis=-1):
    return jax.nn.softmax(x, axis=axis)
def _gelu(x):
    return jax.nn.gelu(x, approximate=True)
def _silu(x):
    return jax.nn.silu(x)
def _sigmoid(x):
    return jax.nn.sigmoid(x)
def _layernorm(x, axis=-1, eps=1e-5):
    m = jnp.mean(x, axis=axis, keepdims=True)
    v = jnp.var(x, axis=axis, keepdims=True)
    return (x - m) / jnp.sqrt(v + eps)
def _scatter_add(tgt, idx, src, axis=0):
    return tgt.at[idx].add(src)
def _segment_sum(src, seg, n):
    return jax.ops.segment_sum(src, seg, n)

kernel_name = 'mk_conv_seq_d2_conv_nchw512_0d2925'

def setup_inputs(seed: int = 0):
    np.random.seed(seed)
    _w = jnp.asarray
    def _rec_inputs():
        import jax
        import jax.numpy as jnp
        _gk = jax.random.key(seed)
        x = 7.22e-05 + 1 * jax.random.normal(jax.random.fold_in(_gk, 1), (4, 512, 64, 64), jnp.float32)
        return x
    x = _rec_inputs()
    def _L0_conv_setup():
        import jax, jax.numpy as jnp
        import numpy as np
        B, C, H, W = (4, 512, 64, 64)
        CI = C // 4
        key = jax.random.key(seed)
        ks = jax.random.split(key, 9)
        s = 1.0 / np.sqrt(C)
        si = 1.0 / np.sqrt(CI)
        return {'x': jax.random.normal(ks[0], (B, C, H, W), dtype=jnp.float32), 'wq': jax.random.uniform(ks[1], (CI, C), jnp.float32, -s, s), 'bq': jax.random.uniform(ks[2], (CI,), jnp.float32, -s, s), 'wk': jax.random.uniform(ks[3], (CI, C), jnp.float32, -s, s), 'bk': jax.random.uniform(ks[4], (CI,), jnp.float32, -s, s), 'wv': jax.random.uniform(ks[5], (CI, C), jnp.float32, -s, s), 'bv': jax.random.uniform(ks[6], (CI,), jnp.float32, -s, s), 'wo': jax.random.uniform(ks[7], (C, CI), jnp.float32, -si, si), 'bo': jax.random.uniform(ks[8], (C,), jnp.float32, -si, si)}
    _L0_conv_all = _L0_conv_setup()
    _L0_conv_in = {k: v for k, v in _L0_conv_all.items() if k in ('wq', 'bq', 'wk', 'bk', 'wv', 'bv', 'wo', 'bo', )}
    del _L0_conv_all

    def _L1_conv_setup():
        import jax, jax.numpy as jnp
        import numpy as np
        CB = 4
        CD = 128
        key = jax.random.key(seed)
        kx, kw = jax.random.split(key)
        x = jax.random.normal(kx, (8, 512, 128, 128), dtype=jnp.float32)
        wc = jax.random.normal(kw, (CB, CD, CD), dtype=jnp.float32) * 0.02
        return {'x': x, 'wc': wc}
    _L1_conv_all = _L1_conv_setup()
    _L1_conv_in = {k: v for k, v in _L1_conv_all.items() if k in ('wc', )}
    del _L1_conv_all

    return {
        "x": x,
        "L0_conv_wq": _L0_conv_in["wq"],
        "L0_conv_bq": _L0_conv_in["bq"],
        "L0_conv_wk": _L0_conv_in["wk"],
        "L0_conv_bk": _L0_conv_in["bk"],
        "L0_conv_wv": _L0_conv_in["wv"],
        "L0_conv_bv": _L0_conv_in["bv"],
        "L0_conv_wo": _L0_conv_in["wo"],
        "L0_conv_bo": _L0_conv_in["bo"],
        "L1_conv_wc": _L1_conv_in["wc"],
    }

def reference(x, L0_conv_wq, L0_conv_bq, L0_conv_wk, L0_conv_bk, L0_conv_wv, L0_conv_bv, L0_conv_wo, L0_conv_bo, L1_conv_wc):
    import jax
    import jax.numpy as jnp
    def _L0_conv_ref(x, wq, bq, wk, bk, wv, bv, wo, bo):
        import jax, jax.numpy as jnp
        import numpy as np
        B, C, H, W = (4, 512, 64, 64)
        CI = C // 4
        b, c, h, w = x.shape
        n = h * w
        xf = x.reshape(b, c, n)
        q = jnp.einsum('oc,bcn->bon', wq, xf) + bq[:, None]
        k = jnp.einsum('oc,bcn->bon', wk, xf) + bk[:, None]
        v = jnp.einsum('oc,bcn->bon', wv, xf) + bv[:, None]
        energy = jnp.einsum('bci,bcj->bij', q, k)
        attn = jax.nn.softmax(energy, axis=-1)
        out = jnp.einsum('bcj,bij->bci', v, attn)
        out = jnp.einsum('oc,bcn->bon', wo, out) + bo[:, None]
        out = out.reshape(b, c, h, w) + x
        return out

    def _L1_conv_ref(x, wc):
        import jax, jax.numpy as jnp
        import numpy as np
        CB = 4
        CD = 128
        B, C, H, W = x.shape
        xr = jnp.transpose(x, (0, 2, 3, 1)).reshape(B, H, W, CB, CD)
        out = jnp.einsum('bhwij,ijk->bhwik', xr, wc)
        out = out.reshape(B, H, W, C).transpose(0, 3, 1, 2)
        return jax.nn.gelu(x + out, approximate=False)

    def _gn(v, G=32, eps=1e-5):
        B_, C_, H_, W_ = v.shape
        g = v.reshape(B_, G, C_ // G, H_, W_)
        m = jnp.mean(g, axis=(2, 3, 4), keepdims=True)
        s = jnp.var(g, axis=(2, 3, 4), keepdims=True)
        return ((g - m) / jnp.sqrt(s + eps)).reshape(v.shape)

    def _ln_c(v, eps=1e-6):
        m = jnp.mean(v, axis=1, keepdims=True)
        s = jnp.var(v, axis=1, keepdims=True)
        return (v - m) / jnp.sqrt(s + eps)

    def _ln_t(v, eps=1e-5):
        m = jnp.mean(v, axis=-1, keepdims=True)
        s = jnp.var(v, axis=-1, keepdims=True)
        return (v - m) / jnp.sqrt(s + eps)

    def _to_tokens(v):
        B_, C_, H_, W_ = v.shape
        return v.reshape(B_, C_, H_ * W_).transpose(0, 2, 1)
    def _from_tokens(t, like):
        B_, C_, H_, W_ = like.shape
        return t.transpose(0, 2, 1).reshape(B_, C_, H_, W_)

    x = _L0_conv_ref(x, L0_conv_wq, L0_conv_bq, L0_conv_wk, L0_conv_bk, L0_conv_wv, L0_conv_bv, L0_conv_wo, L0_conv_bo)
    x = _L1_conv_ref(x, L1_conv_wc)
    return x


_drawn_inputs = setup_inputs


def setup_inputs(seed=0):
    import zlib

    import numpy as np

    out = dict(_drawn_inputs(seed))
    spreads = {}
    factors = {'L0_conv_bq': 4.046, 'L0_conv_bk': 8.0, 'L0_conv_bv': 3.607}
    for name, (base, spread) in spreads.items():
        noise = np.random.default_rng([zlib.crc32(name.encode()), seed]).standard_normal(out[name].shape)
        drawn = base * np.exp(spread * noise) if base else spread * noise
        out[name] = jnp.asarray(drawn.astype(out[name].dtype))
    for name, factor in factors.items():
        out[name] = (out[name] * factor).astype(out[name].dtype)
    return out
```

```python
import concourse.bass as bass
from concourse import mybir
from contextlib import ExitStack


def attention_conv_kernel(nc: bass.Bass, x: bass.AP, wq: bass.AP, bq: bass.AP, wk: bass.AP,
                          bk: bass.AP, wv: bass.AP, bv: bass.AP, wo: bass.AP, bo: bass.AP,
                          wc: bass.AP, out: bass.AP):
    fp32 = mybir.dt.float32
    fp32r = mybir.dt.float32r
    ALU = mybir.AluOpType
    ACT = mybir.ActivationFunctionType
    AX = mybir.AxisListType

    B, C, H, W = x.shape
    N = H * W
    P = 128
    CT = C // P
    QC = 512
    CHUNKS = N // QC
    PAIRS = N // P // 2
    PT = QC // P
    RING = 4
    assert wq.shape[0] == P and wc.shape[1] == P and CHUNKS % 2 == 0

    x_v = x.rearrange("b (c p) h w -> p b c (h w)", p=P)
    out_v = out.rearrange("b (c p) h w -> p b c (h w)", p=P)

    ctx = ExitStack()
    with ctx:
        def sb(name, shape, dt=fp32):
            return ctx.enter_context(nc.sbuf_tensor(name, shape, dt))

        def sem(name):
            return ctx.enter_context(nc.semaphore(name))

        w_nat = sb("w_nat", [P, 3, C])
        wT = sb("wT", [P, 3, CT, P])
        wo_sb = sb("wo_sb", [P, CT, P])
        M_sb = sb("M_sb", [P, CT, P])
        woM = sb("woM", [P, CT, P])
        bq_c = sb("bq_c", [P, 1])
        bk_c = sb("bk_c", [P, 1])
        bv_row = sb("bv_row", [1, P])
        bv_all = sb("bv_all", [P, P])
        bo_c = sb("bo_c", [P, CT])
        boM = sb("boM", [P, CT])
        ident = sb("ident", [P, P])
        ones = sb("ones", [P, P])
        x_a = sb("x_a", [P, CT, QC])
        x_b = sb("x_b", [P, CT, QC])
        k_hi = sb("k_hi", [P, N], fp32r)
        k_lo = sb("k_lo", [P, N], fp32r)
        v_sb = sb("v_sb", [P, N // P, P])
        q_hi = sb("q_hi", [P, QC], fp32r)
        q_lo = sb("q_lo", [P, QC], fp32r)
        s_sb = sb("s_sb", [P, PAIRS, 2, QC])
        p_sb = sb("p_sb", [P, RING, 2, QC])
        max_sb = sb("max_sb", [P, QC])
        max_col = sb("max_col", [P, PT])
        max_diag = sb("max_diag", [P, PT, P])
        max_all = sb("max_all", [P, QC])
        sum_sb = sb("sum_sb", [P, QC])
        rsum_all = sb("rsum_all", [P, QC])
        a_sb = sb("a_sb", [P, QC])
        y_sb = sb("y_sb", [P, CT, QC])

        def bank(name, shape):
            return ctx.enter_context(nc.psum_tensor(name, shape, fp32))

        s_ps = bank("s_ps", [P, 2, 2, QC])
        pv_ps = bank("pv_ps", [P, QC])
        maxb_ps = bank("maxb_ps", [P, QC])
        sum_ps = bank("sum_ps", [P, QC])
        max_ps = bank("max_ps", [P, QC])
        q_ps = s_ps[:, 0, 0, :]
        y_ps = [s_ps[:, 0, 1, :], s_ps[:, 1, 0, :], s_ps[:, 1, 1, :], s_ps[:, 0, 0, :]]
        max_t = max_ps[:, :].rearrange("p (k j) -> p k j", k=PT)

        w_loaded = sem("w_loaded")
        consts_ready = sem("consts_ready")
        ident_zero = sem("ident_zero")
        m_ready = sem("m_ready")
        setup_ps = sem("setup_ps")
        setup_saved = sem("setup_saved")
        xkv_a = sem("xkv_a")
        xkv_b = sem("xkv_b")
        xq_loaded = sem("xq_loaded")
        xy_loaded = sem("xy_loaded")
        y_stored = sem("y_stored")
        k_ready = sem("k_ready")
        k_hi_done = sem("k_hi_done")
        k_lo_done = sem("k_lo_done")
        v_ready = sem("v_ready")
        v_saved = sem("v_saved")
        q_ready = sem("q_ready")
        q_hi_done = sem("q_hi_done")
        q_lo_done = sem("q_lo_done")
        s_ready = sem("s_ready")
        s_saved = sem("s_saved")
        max_done = sem("max_done")
        maxt_ready = sem("maxt_ready")
        maxcol_done = sem("maxcol_done")
        diag_done = sem("diag_done")
        maxb_ready = sem("maxb_ready")
        maxb_saved = sem("maxb_saved")
        sub_done = sem("sub_done")
        exp_done = sem("exp_done")
        pv_done = sem("pv_done")
        sum_done = sem("sum_done")
        sumb_ready = sem("sumb_ready")
        rsum_done = sem("rsum_done")
        a_done = sem("a_done")
        yx_done = sem("yx_done")
        y_ready = sem("y_ready")
        y_saved = sem("y_saved")

        SETUP_STEPS = 3 + 1 + CT + 1
        LOADS = 5 + 3 + CT
        LAST = PAIRS - 1
        START = 1
        block = ctx.enter_context(nc.Block())

        @block.sync
        def _(sp):
            sp.sem_inc(y_stored, START)
            for n, w in enumerate((wq, wk, wv)):
                sp.dma_start(w_nat[:, n, :], w).then_inc(w_loaded, 16)
            sp.dma_start(wo_sb[:, :, :], wo.rearrange("(g p) c -> p g c", p=P)).then_inc(w_loaded, 16)
            sp.dma_start(M_sb[:, :, :], wc.rearrange("g j k -> j g k")).then_inc(w_loaded, 16)
            sp.dma_start(bq_c[:, :], bq.rearrange("(p a) -> p a", a=1)).then_inc(w_loaded, 16)
            sp.dma_start(bk_c[:, :], bk.rearrange("(p a) -> p a", a=1)).then_inc(w_loaded, 16)
            sp.dma_start(bv_row[:, :], bv.rearrange("(a p) -> a p", a=1)).then_inc(w_loaded, 16)
            for g in range(CT):
                sp.dma_start(bo_c[:, g:g + 1], bo[g * P:(g + 1) * P].rearrange("(p a) -> p a", a=1))\
                  .then_inc(w_loaded, 16)

            def x_chunk(b, t):
                return x_v[:, bass.ds(b, 1), :, bass.ds(t * QC, QC)].rearrange("p a c n -> p (a c) n")

            def load_q(b, t, g):
                if g is not None:
                    sp.wait_ge(q_ready, START + g)
                sp.dma_start(x_a[:, :, :], x_chunk(b, t)).then_inc(xq_loaded, 16)

            def load_y(b, t, g):
                if g is not None:
                    sp.wait_ge(yx_done, START + g)
                sp.dma_start(x_b[:, :, :], x_chunk(b, t)).then_inc(xy_loaded, 16)

            def store(b, t, g):
                sp.wait_ge(y_saved, START + CT * (g + 1))
                sp.dma_start(out_v[:, bass.ds(b, 1), :, bass.ds(t * QC, QC)]
                             .rearrange("p a c n -> p (a c) n"), y_sb[:, :, :]).then_inc(y_stored, 16)

            with sp.Fori(0, B) as b:
                g0 = b * CHUNKS
                sp.wait_ge(q_ready, START + g0)
                sp.dma_start(x_a[:, :, :], x_chunk(b, 0)).then_inc(xkv_a, 16)
                sp.wait_ge(yx_done, START + g0)
                sp.dma_start(x_b[:, :, :], x_chunk(b, 1)).then_inc(xkv_b, 16)
                for n in range(2, CHUNKS, 2):
                    sp.wait_ge(v_ready, g0 + n - 1)
                    sp.dma_start(x_a[:, :, :], x_chunk(b, n)).then_inc(xkv_a, 16)
                    sp.wait_ge(v_ready, g0 + n)
                    sp.dma_start(x_b[:, :, :], x_chunk(b, n + 1)).then_inc(xkv_b, 16)
                sp.wait_ge(v_ready, g0 + CHUNKS - 1)
                load_q(b, 0, None)
                sp.wait_ge(v_ready, g0 + CHUNKS)
                load_y(b, 0, None)
                load_q(b, 1, g0 + 1)
                with sp.Fori(0, CHUNKS - 2) as t:
                    g = g0 + t
                    load_q(b, t + 2, g + 2)
                    load_y(b, t + 1, g + 1)
                    store(b, t, g)
                load_y(b, CHUNKS - 1, g0 + CHUNKS - 1)
                store(b, CHUNKS - 2, g0 + CHUNKS - 2)
                store(b, CHUNKS - 1, g0 + CHUNKS - 1)
            sp.wait_ge(y_stored, START + 16 * B * CHUNKS)

        @block.tensor
        def _(pe):
            pe.sem_inc(q_ready, START)
            pe.sem_inc(yx_done, START)
            pe.wait_ge(w_loaded, 16 * LOADS)
            pe.wait_ge(consts_ready, 2)
            for n in range(3):
                if n:
                    pe.wait_ge(setup_saved, n)
                for c in range(CT):
                    mm = pe.transpose(max_ps[:, c * P:(c + 1) * P], w_nat[:, n, c * P:(c + 1) * P],
                                      ident[:, :])
                mm.then_inc(setup_ps, 1)
            pe.wait_ge(setup_saved, 3)
            pe.matmul(max_ps[:, 0:P], ones[0:1, :], bv_row[:, :], start=True, stop=True)\
              .then_inc(setup_ps, 1)
            pe.wait_ge(m_ready, 1)
            for g in range(CT):
                pe.wait_ge(setup_saved, 4 + g)
                pe.matmul(max_ps[:, 0:P], wo_sb[:, g, :], M_sb[:, g, :], start=True, stop=True)\
                  .then_inc(setup_ps, 1)
            pe.wait_ge(setup_saved, 4 + CT)
            for g in range(CT):
                mm = pe.matmul(max_ps[:, g:g + 1], M_sb[:, g, :], bo_c[:, g:g + 1], start=True, stop=True)
            mm.then_inc(setup_ps, 1)
            pe.wait_ge(setup_saved, SETUP_STEPS)

            def keys_values(u, n, xs):
                pe.wait_ge(k_lo_done, START + n)
                for c in range(CT):
                    mm = pe.matmul(s_ps[:, u, 0, :], wT[:, 1, c, :], xs[:, c, :],
                                   start=(c == 0), stop=(c == CT - 1))
                mm.then_inc(k_ready, 1)
                pe.wait_ge(v_saved, START + n)
                for k in range(PT):
                    for c in range(CT):
                        mm = pe.matmul(s_ps[:, u, 1, k * P:(k + 1) * P], xs[:, c, k * P:(k + 1) * P],
                                       wT[:, 2, c, :], start=(c == 0), stop=(c == CT - 1))
                mm.then_inc(v_ready, 1)

            def queries(g):
                pe.wait_ge(xq_loaded, 16 * (g + 1))
                for c in range(CT):
                    mm = pe.matmul(q_ps, wT[:, 0, c, :], x_a[:, c, :], start=(c == 0), stop=(c == CT - 1))
                mm.then_inc(q_ready, 1)

            def scores(p, g):
                if p >= 2:
                    pe.wait_ge(s_saved, PAIRS * g + p - 1)
                for h in range(2):
                    key = (2 * p + h) * P
                    o = s_ps[:, p % 2, h, :]
                    pe.matmul(o, k_lo[:, key:key + P], q_hi[:, :], start=True, stop=False)
                    pe.matmul(o, k_hi[:, key:key + P], q_lo[:, :], start=False, stop=False)
                    mm = pe.matmul(o, k_hi[:, key:key + P], q_hi[:, :], start=False, stop=True)
                mm.then_inc(s_ready, 1)

            def values(p, g):
                pe.wait_ge(exp_done, PAIRS * g + p + 1)
                for h in range(2):
                    mm = pe.matmul(pv_ps[:, :], v_sb[:, 2 * p + h, :], p_sb[:, p % RING, h, :],
                                   start=(p == 0 and h == 0), stop=(p == LAST and h == 1))
                mm.then_inc(pv_done, 1)

            def max_transpose(g):
                pe.wait_ge(max_done, 2 * PAIRS * (g + 1))
                for k in range(PT):
                    mm = pe.transpose(max_t[:, k, :], max_sb[:, k * P:(k + 1) * P], ident[:, :])
                mm.then_inc(maxt_ready, 1)

            def max_broadcast(g):
                pe.wait_ge(diag_done, g + 1)
                pe.matmul(maxb_ps[:, :], ones[:, :], max_diag[:, :, :].rearrange("p k j -> p (k j)"),
                          start=True, stop=True).then_inc(maxb_ready, 1)

            def sum_broadcast(g):
                pe.wait_ge(sum_done, 2 * PAIRS * (g + 1))
                pe.matmul(sum_ps[:, :], ones[:, :], sum_sb[:, :], start=True, stop=True)\
                  .then_inc(sumb_ready, 1)

            def chunk(g, ahead, project):
                if ahead:
                    pe.wait_ge(q_lo_done, g + 2)
                    pe.wait_ge(y_saved, START + CT * g)
                pe.wait_ge(a_done, START + g)
                for p in range(PAIRS):
                    if ahead:
                        scores(p, g + 1)
                    if p:
                        values(p - 1, g)
                if project:
                    pe.wait_ge(s_saved, PAIRS * (g + 2) - 1)
                    queries(g + 2)
                values(LAST, g)
                if ahead:
                    max_transpose(g + 1)
                sum_broadcast(g)
                pe.wait_ge(xy_loaded, 16 * (g + 1))
                if ahead:
                    pe.wait_ge(s_saved, PAIRS * (g + 2))
                pe.matmul(y_ps[0], M_sb[:, 0, :], x_b[:, 0, :], start=True, stop=False)
                if ahead:
                    max_broadcast(g + 1)
                if project:
                    pe.wait_ge(q_lo_done, g + 3)
                for c in range(1, CT):
                    mm = pe.matmul(y_ps[c], M_sb[:, c, :], x_b[:, c, :], start=True, stop=False)
                mm.then_inc(yx_done, 1)
                pe.wait_ge(a_done, START + g + 1)
                for c in range(CT):
                    pe.matmul(y_ps[c], woM[:, c, :], a_sb[:, :], start=False, stop=True)\
                      .then_inc(y_ready, 1)

            with pe.Fori(0, B) as b:
                g0 = b * CHUNKS
                with pe.Fori(0, CHUNKS // 2) as i:
                    n = g0 + 2 * i
                    pe.wait_ge(y_saved, START + CT * g0)
                    pe.wait_ge(xkv_a, (b * (CHUNKS // 2) + i + 1) * 16)
                    keys_values(0, n, x_a)
                    pe.wait_ge(xkv_b, (b * (CHUNKS // 2) + i + 1) * 16)
                    keys_values(1, n + 1, x_b)
                pe.wait_ge(k_lo_done, START + g0 + CHUNKS)
                pe.wait_ge(v_saved, START + g0 + CHUNKS)
                queries(g0)
                pe.wait_ge(q_lo_done, g0 + 1)
                for p in range(PAIRS):
                    scores(p, g0)
                pe.wait_ge(s_saved, PAIRS * (g0 + 1) - 1)
                queries(g0 + 1)
                max_transpose(g0)
                max_broadcast(g0)
                with pe.Fori(0, CHUNKS - 2) as t:
                    chunk(g0 + t, True, True)
                chunk(g0 + CHUNKS - 2, True, False)
                chunk(g0 + CHUNKS - 1, False, False)

        @block.scalar
        def _(act):
            act.sem_inc(y_saved, START)
            def keys(u, n, i):
                act.wait_ge(k_ready, n + 1)
                act.activation(k_hi[:, bass.ds((2 * i + u) * QC, QC)], s_ps[:, u, 0, :], ACT.Identity,
                               bias=bk_c[:, :]).then_inc(k_hi_done, 1)

            def queries(g):
                act.wait_ge(q_ready, START + g + 1)
                act.activation(q_hi[:, :], q_ps, ACT.Identity, bias=bq_c[:, :]).then_inc(q_hi_done, 1)

            def scores(p, g, over=None):
                act.wait_ge(s_ready, PAIRS * g + p + 1)
                if over is not None:
                    act.wait_ge(exp_done, PAIRS * over + p + 1)
                act.activation(s_sb[:, p, :, :], s_ps[:, p % 2, :, :], ACT.Copy).then_inc(s_saved, 1)

            def exps(p, g):
                act.wait_ge(sub_done, PAIRS * g + p + 1)
                if p >= RING:
                    act.wait_ge(pv_done, PAIRS * g + p - RING + 1)
                    act.wait_ge(sum_done, 2 * (PAIRS * g + p - RING + 1))
                act.activation(p_sb[:, p % RING, :, :], s_sb[:, p, :, :], ACT.Exp).then_inc(exp_done, 1)

            def max_broadcast(g):
                act.wait_ge(maxb_ready, g + 1)
                act.activation(max_all[:, :], maxb_ps[:, :], ACT.Copy).then_inc(maxb_saved, 1)

            def chunk(g, ahead, project):
                for p in range(PAIRS):
                    exps(p, g)
                    if ahead:
                        scores(p, g + 1, over=g)
                if project:
                    queries(g + 2)
                if ahead:
                    max_broadcast(g + 1)
                act.wait_ge(y_stored, START + 16 * g)
                for c in range(CT):
                    act.wait_ge(y_ready, CT * g + c + 1)
                    act.activation(y_sb[:, c, :], y_ps[c], ACT.Gelu, bias=boM[:, c:c + 1])\
                       .then_inc(y_saved, 1)

            act.wait_ge(setup_saved, SETUP_STEPS)
            with act.Fori(0, B) as b:
                g0 = b * CHUNKS
                with act.Fori(0, CHUNKS // 2) as i:
                    keys(0, g0 + 2 * i, i)
                    keys(1, g0 + 2 * i + 1, i)
                queries(g0)
                for p in range(PAIRS):
                    scores(p, g0)
                queries(g0 + 1)
                max_broadcast(g0)
                with act.Fori(0, CHUNKS - 2) as t:
                    chunk(g0 + t, True, True)
                chunk(g0 + CHUNKS - 2, True, False)
                chunk(g0 + CHUNKS - 1, False, False)

        @block.gpsimd
        def _(pool):
            pool.memset(ones[:, :], 1.0).then_inc(consts_ready, 1)
            pool.memset(ident[:, :], 0.0).then_inc(ident_zero, 1)
            pool.wait_ge(ident_zero, 1)
            pool.affine_select(out=ident[:, :], in_=ident[:, :], compare_op=ALU.not_equal, fill=1.0,
                               base=0, pattern=[[-1, P]], channel_multiplier=1).then_inc(consts_ready, 1)
            with pool.Fori(0, B * CHUNKS) as g:
                pool.wait_ge(maxb_saved, g + 1)
                for p in range(PAIRS):
                    pool.tensor_tensor(s_sb[:, p, :, :], s_sb[:, p, :, :],
                                       max_all[:, None, :].broadcast_to([P, 2, QC]), ALU.subtract)\
                        .then_inc(sub_done, 1)

        @block.vector
        def _(dve):
            for free in (k_lo_done, v_saved, a_done):
                dve.sem_inc(free, START)
            dve.wait_ge(consts_ready, 2)
            dve.wait_ge(w_loaded, 16 * LOADS)
            for g in range(CT):
                add = dve.tensor_tensor(M_sb[:, g, :], M_sb[:, g, :], ident[:, :], ALU.add)
            add.then_inc(m_ready, 1)
            for n in range(3):
                dve.wait_ge(setup_ps, n + 1)
                dve.tensor_copy(wT[:, n, :, :].rearrange("p c o -> p (c o)"), max_ps[:, :])\
                   .then_inc(setup_saved, 1)
            dve.wait_ge(setup_ps, 4)
            dve.tensor_copy(bv_all[:, :], max_ps[:, 0:P]).then_inc(setup_saved, 1)
            for g in range(CT):
                dve.wait_ge(setup_ps, 5 + g)
                dve.tensor_copy(woM[:, g, :], max_ps[:, 0:P]).then_inc(setup_saved, 1)
            dve.wait_ge(setup_ps, 5 + CT)
            dve.tensor_copy(boM[:, :], max_ps[:, 0:CT]).then_inc(setup_saved, 1)
            dve.wait_ge(setup_saved, SETUP_STEPS)

            def keys(u, n, i):
                dve.wait_ge(k_hi_done, n + 1)
                cols = bass.ds((2 * i + u) * QC, QC)
                dve.scalar_tensor_tensor(out=k_lo[:, cols], in0=s_ps[:, u, 0, :], scalar=bk_c[:, :],
                                         in1=k_hi[:, cols].bitcast(fp32), op0=ALU.add,
                                         op1=ALU.subtract).then_inc(k_lo_done, 1)

            def values(u, n, i):
                dve.wait_ge(v_ready, n + 1)
                dve.tensor_tensor(v_sb[:, bass.ds((2 * i + u) * PT, PT), :],
                                  s_ps[:, u, 1, :].rearrange("p (k c) -> p k c", k=PT),
                                  bv_all[:, None, :].broadcast_to([P, PT, P]), ALU.add).then_inc(v_saved, 1)

            def queries(g):
                dve.wait_ge(q_hi_done, g + 1)
                dve.scalar_tensor_tensor(out=q_lo[:, :], in0=q_ps, scalar=bq_c[:, :],
                                         in1=q_hi[:, :].bitcast(fp32), op0=ALU.add,
                                         op1=ALU.subtract).then_inc(q_lo_done, 1)

            def running_max(p, h, g):
                if h == 0:
                    dve.wait_ge(s_saved, PAIRS * g + p + 1)
                tile = s_sb[:, p, h, :]
                if p == 0 and h == 0:
                    dve.tensor_copy(max_ps[:, :], tile).then_inc(max_done, 1)
                    return
                dve.wait_ge(max_done, 2 * (PAIRS * g + p) + h)
                to = max_sb if (p == LAST and h == 1) else max_ps
                dve.tensor_tensor(to[:, :], tile, max_ps[:, :], ALU.max).then_inc(max_done, 1)

            def running_sum(p, h, g):
                if h == 0:
                    dve.wait_ge(exp_done, PAIRS * g + p + 1)
                tile = p_sb[:, p % RING, h, :]
                if p == 0 and h == 0:
                    dve.tensor_copy(sum_ps[:, :], tile).then_inc(sum_done, 1)
                    return
                dve.wait_ge(sum_done, 2 * (PAIRS * g + p) + h)
                to = sum_sb if (p == LAST and h == 1) else sum_ps
                dve.tensor_tensor(to[:, :], tile, sum_ps[:, :], ALU.add).then_inc(sum_done, 1)

            def max_columns(g):
                dve.wait_ge(maxt_ready, g + 1)
                dve.tensor_reduce(max_col[:, :], max_t, AX.X, ALU.max).then_inc(maxcol_done, 1)
                dve.wait_ge(maxcol_done, g + 1)
                for k in range(PT):
                    put = dve.tensor_scalar(max_diag[:, k, :], ident[:, :], max_col[:, k:k + 1], None,
                                            ALU.mult)
                put.then_inc(diag_done, 1)

            def normalise(g):
                dve.wait_ge(sumb_ready, g + 1)
                dve.reciprocal(rsum_all[:, :], sum_ps[:, :]).then_inc(rsum_done, 1)
                dve.wait_ge(rsum_done, g + 1)
                dve.wait_ge(pv_done, PAIRS * (g + 1))
                dve.tensor_tensor(a_sb[:, :], pv_ps[:, :], rsum_all[:, :], ALU.mult).then_inc(a_done, 1)

            def chunk(g, ahead, project):
                for p in range(PAIRS):
                    for h in range(2):
                        running_sum(p, h, g)
                        if ahead:
                            running_max(p, h, g + 1)
                if project:
                    queries(g + 2)
                if ahead:
                    max_columns(g + 1)
                normalise(g)

            with dve.Fori(0, B) as b:
                g0 = b * CHUNKS
                with dve.Fori(0, CHUNKS // 2) as i:
                    for u in range(2):
                        keys(u, g0 + 2 * i + u, i)
                        values(u, g0 + 2 * i + u, i)
                queries(g0)
                for p in range(PAIRS):
                    for h in range(2):
                        running_max(p, h, g0)
                queries(g0 + 1)
                max_columns(g0)
                with dve.Fori(0, CHUNKS - 2) as t:
                    chunk(g0 + t, True, True)
                chunk(g0 + CHUNKS - 2, True, False)
                chunk(g0 + CHUNKS - 1, False, False)


_INS = ["x", "L0_conv_wq", "L0_conv_bq", "L0_conv_wk", "L0_conv_bk", "L0_conv_wv", "L0_conv_bv",
        "L0_conv_wo", "L0_conv_bo", "L1_conv_wc"]


def kernel(**inputs):
    import numpy as _np
    import concourse.bacc as _bacc
    from concourse import mybir as _mybir
    from concourse.bass_utils import run_bass_kernel_spmd as _run

    nc = _bacc.Bacc("TRN2", target_bir_lowering=False, num_devices=1)
    arrays, args = {}, []
    for name in _INS:
        a = _np.ascontiguousarray(inputs[name])
        arrays[f"in_{name}_dram"] = a
        args.append(nc.dram_tensor(f"in_{name}_dram", a.shape, _mybir.dt.from_np(a.dtype),
                                   kind="ExternalInput").ap())
    shape = tuple(inputs["x"].shape)
    out = nc.dram_tensor("out_dram", shape, _mybir.dt.float32, kind="ExternalOutput").ap()
    attention_conv_kernel(nc, *args, out)
    r = _run(nc, [arrays], core_ids=[0])
    return r.results[0]["out_dram"]
```

```python
import concourse.bass as bass
from concourse import mybir
from contextlib import ExitStack


def attention_conv_kernel(nc: bass.Bass, x: bass.AP, wq: bass.AP, bq: bass.AP, wk: bass.AP,
                          bk: bass.AP, wv: bass.AP, bv: bass.AP, wo: bass.AP, bo: bass.AP,
                          wc: bass.AP, out: bass.AP):
    fp32 = mybir.dt.float32
    fp32r = mybir.dt.float32r
    ALU = mybir.AluOpType
    ACT = mybir.ActivationFunctionType
    AX = mybir.AxisListType

    B, C, H, W = x.shape
    N = H * W
    P = 128
    CT = C // P
    QC = 512
    CHUNKS = N // QC
    PAIRS = N // P // 2
    PT = QC // P
    RING = 4
    SPLIT_AT = PAIRS // 2 - 2
    assert wq.shape[0] == P and wc.shape[1] == P and PAIRS == 2 * CHUNKS and PAIRS >= 8

    x_v = x.rearrange("b (c p) h w -> p b c (h w)", p=P)
    out_v = out.rearrange("b (c p) h w -> p b c (h w)", p=P)

    ctx = ExitStack()
    with ctx:
        def sb(name, shape, dt=fp32):
            return ctx.enter_context(nc.sbuf_tensor(name, shape, dt))

        def sem(name):
            return ctx.enter_context(nc.semaphore(name))

        wT_hi = sb("wT_hi", [P, 2, CT, P], fp32r)
        wT_lo = sb("wT_lo", [P, 2, CT, P], fp32r)
        wvT = sb("wvT", [P, CT, P])
        M_sb = sb("M_sb", [P, CT, P])
        woM = sb("woM", [P, CT, P])
        bq_c = sb("bq_c", [P, 1])
        bk_c = sb("bk_c", [P, 1])
        bv_c = sb("bv_c", [P, 1])
        bo_c = sb("bo_c", [P, CT])
        y_bias = sb("y_bias", [P, CT])
        ident = sb("ident", [P, P])
        ones = sb("ones", [P, P])
        s_sb = sb("s_sb", [P, PAIRS, 2, QC])
        w_nat = s_sb[:, PAIRS - 2:PAIRS, :, :].rearrange("p a b n -> p (a b) n")
        wo_nat = w_nat[:, 3, :].rearrange("p (g c) -> p g c", g=CT)
        x_raw = sb("x_raw", [P, CT, QC])
        xs_hi = sb("xs_hi", [P, CT, QC], fp32r)
        xs_lo = sb("xs_lo", [P, CT, QC], fp32r)
        k_hi = sb("k_hi", [P, N], fp32r)
        k_lo = sb("k_lo", [P, N], fp32r)
        v_nat = sb("v_nat", [P, PAIRS, P])
        v_hi = sb("v_hi", [P, PAIRS, P], fp32r)
        v_lo = sb("v_lo", [P, PAIRS, P], fp32r)
        q_hi = sb("q_hi", [P, QC], fp32r)
        q_lo = sb("q_lo", [P, QC], fp32r)
        p_nat = sb("p_nat", [P, RING, QC])
        p_hi = sb("p_hi", [P, RING, QC], fp32r)
        p_lo = sb("p_lo", [P, RING, QC], fp32r)
        max_sb = sb("max_sb", [P, QC])
        max_col = sb("max_col", [P, PT])
        max_all = sb("max_all", [P, QC])
        sum_sb = sb("sum_sb", [P, QC])
        sum2_sb = sb("sum2_sb", [P, QC])
        rsum_all = sb("rsum_all", [P, QC])
        max_diag = sb("max_diag", [P, PT, P])
        a_sb = sb("a_sb", [P, QC])

        def bank(name, shape):
            return ctx.enter_context(nc.psum_tensor(name, shape, fp32))

        s_ps = bank("s_ps", [P, 2, 2, QC])
        pv_ps = bank("pv_ps", [P, QC])
        p_ps = bank("p_ps", [P, QC])
        sum_ps = bank("sum_ps", [P, QC])
        max_ps = bank("max_ps", [P, QC])
        q_ps = s_ps[:, 0, 0, :]
        q0_ps = s_ps[:, 1, 0, :]
        y_ps = [s_ps[:, 0, 1, :], s_ps[:, 1, 0, :], s_ps[:, 0, 0, :], s_ps[:, 1, 1, :]]
        max_t = max_ps[:, :].rearrange("p (k j) -> p k j", k=PT)

        w_loaded = sem("w_loaded")
        consts_ready = sem("consts_ready")
        ident_zero = sem("ident_zero")
        m_ready = sem("m_ready")
        setup_ps = sem("setup_ps")
        setup_hi = sem("setup_hi")
        setup_saved = sem("setup_saved")
        xkv_loaded = [sem(f"xkv_loaded{t}") for t in range(CHUNKS)]
        xq_loaded = sem("xq_loaded")
        xy_loaded = sem("xy_loaded")
        y_stored = sem("y_stored")
        xkv_hi = sem("xkv_hi")
        xkv_lo = sem("xkv_lo")
        xkv_used = sem("xkv_used")
        k_hi_done = sem("k_hi_done")
        k_lo_done = sem("k_lo_done")
        v_ready = sem("v_ready")
        v_hi_done = sem("v_hi_done")
        v_lo_done = sem("v_lo_done")
        v_nat_done = sem("v_nat_done")
        xq_hi = sem("xq_hi")
        xq_lo = sem("xq_lo")
        q_ready = sem("q_ready")
        q_hi_done = sem("q_hi_done")
        q_lo_done = sem("q_lo_done")
        s_ready = sem("s_ready")
        s_saved = sem("s_saved")
        max_done = sem("max_done")
        maxt_ready = sem("maxt_ready")
        maxcol_done = sem("maxcol_done")
        maxdiag_done = sem("maxdiag_done")
        maxb_ready = sem("maxb_ready")
        maxb_saved = sem("maxb_saved")
        sub_done = sem("sub_done")
        expn_done = sem("expn_done")
        exps_done = sem("exps_done")
        p_lo_done = sem("p_lo_done")
        pv_done = sem("pv_done")
        sum_done = sem("sum_done")
        sum2_done = sem("sum2_done")
        total_done = sem("total_done")
        sumb_ready = sem("sumb_ready")
        rsum_done = sem("rsum_done")
        a_done = sem("a_done")
        y_ready = sem("y_ready")
        y_saved = sem("y_saved")

        SETUP_STEPS = 3 + CT + 1
        LOADS = 5 + 3 + CT
        LAST = PAIRS - 1
        MAX_LAG = 6

        def renewed_after(p):
            t = (p - 1 - RENEW_LAG) // 2
            return [t] if t >= 0 and (p - 1 - RENEW_LAG) % 2 == 0 else []

        RENEW_LAG = 3
        RENEWED_LAST = [t for t in range(CHUNKS) if 2 * t + 1 + RENEW_LAG > LAST]
        START = CT
        block = ctx.enter_context(nc.Block())


        @block.sync
        def _(sp):
            sp.sem_inc(y_stored, START)
            for n, w in enumerate((wq, wk, wv)):
                sp.dma_start(w_nat[:, n, :], w).then_inc(w_loaded, 16)
            sp.dma_start(wo_nat, wo.rearrange("(g p) c -> p g c", p=P)).then_inc(w_loaded, 16)
            sp.dma_start(M_sb[:, :, :], wc.rearrange("g j k -> j g k")).then_inc(w_loaded, 16)
            for column, bias in ((bq_c, bq), (bk_c, bk), (bv_c, bv)):
                sp.dma_start(column[:, :], bias.rearrange("(p a) -> p a", a=1)).then_inc(w_loaded, 16)
            for g in range(CT):
                sp.dma_start(bo_c[:, g:g + 1], bo[g * P:(g + 1) * P].rearrange("(p a) -> p a", a=1))\
                  .then_inc(w_loaded, 16)

            def x_chunk(b, t):
                return x_v[:, bass.ds(b, 1), :, bass.ds(t * QC, QC)].rearrange("p a c n -> p (a c) n")

            def load_kv(b, n):
                sp.dma_start(s_sb[:, 2 * n:2 * n + 2, :, :].rearrange("p a b n -> p (a b) n"),
                             x_chunk(b, n)).then_inc(xkv_loaded[n], 16)

            def load_q(b, t):
                sp.dma_start(x_raw[:, :, :], x_chunk(b, t)).then_inc(xq_loaded, 16)

            def load_y(b, t):
                sp.dma_start(x_raw[:, :, :], x_chunk(b, t)).then_inc(xy_loaded, 16)

            def store(b, t, g):
                sp.wait_ge(y_saved, START + CT * (g + 1))
                sp.dma_start(out_v[:, bass.ds(b, 1), :, bass.ds(t * QC, QC)]
                             .rearrange("p a c n -> p (a c) n"), x_raw[:, :, :]).then_inc(y_stored, 16)

            def image(b, last):
                g0 = b * CHUNKS
                m0 = b * (CHUNKS - 1)
                sp.wait_ge(xq_lo, CT * (m0 + 1))
                sp.wait_ge(y_stored, START + 16 * g0)
                load_q(b, 2)
                with sp.Fori(1, CHUNKS - 2) as t:
                    g = g0 + t
                    sp.wait_ge(xq_lo, CT * (m0 + t + 1))
                    sp.wait_ge(y_stored, START + 16 * (g - 1))
                    load_q(b, t + 2)
                    sp.wait_ge(xq_lo, CT * (m0 + t + 2))
                    load_y(b, t - 1)
                    store(b, t - 1, g - 1)
                for t in range(CHUNKS - 2, CHUNKS):
                    g = g0 + t
                    sp.wait_ge(y_stored, START + 16 * (g - 1))
                    load_y(b, t - 1)
                    if t == CHUNKS - 1 and not last:
                        for n in range(CHUNKS):
                            sp.wait_ge(exps_done, PAIRS * g + 2 * n + 2)
                            load_kv(b + 1, n)
                    store(b, t - 1, g - 1)
                g = g0 + CHUNKS - 1
                sp.wait_ge(y_stored, START + 16 * g)
                if not last:
                    load_q(b + 1, 1)
                    sp.wait_ge(xq_lo, CT * (m0 + CHUNKS))
                load_y(b, CHUNKS - 1)
                store(b, CHUNKS - 1, g)

            for n in range(CHUNKS):
                if n == CHUNKS - 1:
                    sp.wait_ge(setup_saved, SETUP_STEPS)
                load_kv(0, n)
            load_q(0, 1)
            with sp.Fori(0, B - 1) as b:
                image(b, False)
            image(B - 1, True)
            sp.wait_ge(y_stored, START + 16 * B * CHUNKS)

        @block.tensor
        def _(pe):
            pe.sem_inc(q_ready, START)
            pe.sem_inc(y_ready, START)
            pe.wait_ge(w_loaded, 16 * LOADS)
            pe.wait_ge(consts_ready, 2)
            for n in range(3):
                if n:
                    pe.wait_ge(setup_saved, n)
                for c in range(CT):
                    mm = pe.transpose(max_ps[:, c * P:(c + 1) * P], w_nat[:, n, c * P:(c + 1) * P],
                                      ident[:, :])
                mm.then_inc(setup_ps, 1)
            pe.wait_ge(m_ready, 1)
            for g in range(CT):
                pe.wait_ge(setup_saved, 3 + g)
                pe.matmul(max_ps[:, 0:P], wo_nat[:, g, :], M_sb[:, g, :], start=True, stop=True)\
                  .then_inc(setup_ps, 1)
            pe.wait_ge(setup_saved, 3 + CT)
            for g in range(CT):
                pe.matmul(max_ps[:, g:g + 1], woM[:, g, :], bv_c[:, :], start=True, stop=False)
                mm = pe.matmul(max_ps[:, g:g + 1], M_sb[:, g, :], bo_c[:, g:g + 1],
                               start=False, stop=True)
            mm.then_inc(setup_ps, 1)
            pe.wait_ge(setup_saved, SETUP_STEPS)

            def split_product(o, a_lo, a_hi, b_lo, b_hi, start, stop, **more):
                pe.matmul(o, a_lo, b_hi, start=start, stop=False, **more)
                pe.matmul(o, a_hi, b_lo, start=False, stop=False, **more)
                return pe.matmul(o, a_hi, b_hi, start=False, stop=stop, **more)

            def keys_values(t, n):
                u = t % 2
                if t >= 2:
                    pe.wait_ge(k_lo_done, n - 1)
                    pe.wait_ge(v_lo_done, n - 1)
                if t == 0:
                    for c in range(CT):
                        pe.wait_ge(xkv_lo, CT * n + c + 1)
                        mm = split_product(q0_ps, wT_lo[:, 0, c, :], wT_hi[:, 0, c, :], xs_lo[:, c, :],
                                           xs_hi[:, c, :], start=(c == 0), stop=(c == CT - 1))
                    mm.then_inc(q_ready, 1)
                if t == 1:
                    pe.wait_ge(q_lo_done, n)
                for c in range(CT):
                    pe.wait_ge(xkv_lo, CT * n + c + 1)
                    split_product(s_ps[:, u, 0, :], wT_lo[:, 1, c, :], wT_hi[:, 1, c, :], xs_lo[:, c, :],
                                  xs_hi[:, c, :], start=(c == 0), stop=(c == CT - 1))\
                        .then_inc(xkv_used, 1)
                for k in range(PT):
                    for c in range(CT):
                        mm = pe.matmul(s_ps[:, u, 1, k * P:(k + 1) * P],
                                       s_sb[:, 2 * t + c // 2, c % 2, k * P:(k + 1) * P],
                                       wvT[:, c, :], start=(c == 0), stop=(c == CT - 1))
                mm.then_inc(v_ready, 1)

            def queries(m, g):
                for c in range(CT):
                    pe.wait_ge(xq_lo, CT * (m - 1) + c + 1)
                    mm = split_product(q_ps, wT_lo[:, 0, c, :], wT_hi[:, 0, c, :], xs_lo[:, c, :],
                                       xs_hi[:, c, :], start=(c == 0), stop=(c == CT - 1))
                mm.then_inc(q_ready, 1)

            def scores(p, g):
                if p >= 2:
                    pe.wait_ge(s_saved, PAIRS * g + p - 1)
                for h in range(2):
                    keys = slice((2 * p + h) * P, (2 * p + h + 1) * P)
                    mm = split_product(s_ps[:, p % 2, h, :], k_lo[:, keys], k_hi[:, keys],
                                       q_lo[:, :], q_hi[:, :], start=True, stop=True)
                mm.then_inc(s_ready, 1)

            def values(p, g):
                r = p % RING
                pe.wait_ge(expn_done, PAIRS * g + p + 1)
                pe.matmul(pv_ps[:, :], v_nat[:, p, :], p_nat[:, r, :], start=(p == 0), stop=False)
                pe.wait_ge(p_lo_done, PAIRS * g + p + 1)
                split_product(pv_ps[:, :], v_lo[:, p, :], v_hi[:, p, :], p_lo[:, r, :], p_hi[:, r, :],
                              start=False, stop=(p == LAST)).then_inc(pv_done, 1)

            def max_transpose(g):
                pe.wait_ge(max_done, 2 * PAIRS * (g + 1))
                for k in range(PT):
                    mm = pe.transpose(max_t[:, k, :], max_sb[:, k * P:(k + 1) * P], ident[:, :])
                mm.then_inc(maxt_ready, 1)

            def max_broadcast(g):
                pe.wait_ge(maxdiag_done, g + 1)
                pe.matmul(max_ps[:, :], ones[:, :], max_diag[:, :, :].rearrange("p k j -> p (k j)"),
                          start=True, stop=True)\
                  .then_inc(maxb_ready, 1)

            def sum_broadcast(g):
                pe.wait_ge(total_done, g + 1)
                pe.matmul(sum_ps[:, :], ones[:, :], sum_sb[:, :], start=True, stop=True)\
                  .then_inc(sumb_ready, 1)

            def second_layer(c, g):
                if g is not None:
                    if c == 0:
                        pe.wait_ge(xy_loaded, 16 * (g + 1))
                        pe.wait_ge(a_done, START + g + 1)
                    pe.matmul(y_ps[c], M_sb[:, c, :], x_raw[:, c, :], start=True, stop=False)
                    pe.matmul(y_ps[c], woM[:, c, :], a_sb[:, :], start=False, stop=True)\
                      .then_inc(y_ready, 1)

            def between(y, maximum, total, projected):
                second_layer(0, y)
                if total is not None:
                    sum_broadcast(total)
                if maximum is not None:
                    pe.wait_ge(s_saved, PAIRS * (maximum + 1))
                second_layer(1, y)
                if maximum is not None:
                    max_transpose(maximum)
                if projected:
                    pe.wait_ge(q_lo_done, maximum + 2)
                second_layer(2, y)
                if maximum is not None:
                    max_broadcast(maximum)
                second_layer(3, y)

            def chunk(m, g, ahead, project, renew, y):
                if ahead:
                    pe.wait_ge(q_lo_done, g + 2)
                if renew:
                    pe.wait_ge(y_saved, START + CT * (g - 1))
                for p in range(PAIRS):
                    if ahead:
                        if p < 2:
                            pe.wait_ge(y_saved, START + CT * (g - 1 if y else g) - (1 - p))
                        scores(p, g + 1)
                    if p == 1:
                        pe.wait_ge(a_done, START + g)
                    if p:
                        values(p - 1, g)
                        for t in renewed_after(p - 1) if renew else ():
                            keys_values(t, g + 1 + t)
                if ahead or project:
                    pe.wait_ge(s_saved, PAIRS * (g + 2) - 1)
                if project:
                    queries(m + 2, g + 2)
                values(LAST, g)
                if renew:
                    for t in renewed_after(LAST) + RENEWED_LAST:
                        keys_values(t, g + 1 + t)
                    pe.wait_ge(k_lo_done, g + 1 + CHUNKS)
                    pe.wait_ge(v_lo_done, g + 1 + CHUNKS)
                between(g - 1 if y else None, g + 1 if ahead else None, g, project)

            def first_scores(m, g0, y):
                pe.wait_ge(q_lo_done, g0 + 1)
                for p in range(PAIRS):
                    scores(p, g0)
                pe.wait_ge(s_saved, PAIRS * (g0 + 1) - 1)
                queries(m + 1, g0 + 1)
                between(y, g0, None, True)

            def image(b, last):
                g0 = b * CHUNKS
                m0 = b * (CHUNKS - 1)
                chunk(m0, g0, True, True, False, False)
                with pe.Fori(1, CHUNKS - 2) as t:
                    chunk(m0 + t, g0 + t, True, True, False, True)
                chunk(m0 + CHUNKS - 2, g0 + CHUNKS - 2, True, False, False, True)
                chunk(m0 + CHUNKS - 1, g0 + CHUNKS - 1, False, False, not last, True)
                pe.wait_ge(y_saved, START + CT * (g0 + CHUNKS - 1))
                if not last:
                    first_scores(m0 + CHUNKS - 1, g0 + CHUNKS, g0 + CHUNKS - 1)
                else:
                    between(g0 + CHUNKS - 1, None, None, False)

            for t in range(CHUNKS):
                keys_values(t, t)
            pe.wait_ge(k_lo_done, CHUNKS)
            pe.wait_ge(v_lo_done, CHUNKS)
            first_scores(0, 0, None)
            with pe.Fori(0, B - 1) as b:
                image(b, False)
            image(B - 1, True)

        @block.scalar
        def _(act):
            act.sem_inc(y_saved, START)

            def split_x_kv(t, image, n):
                act.wait_ge(xkv_loaded[t], 16 * (image + 1))
                for c in range(CT):
                    if t:
                        act.wait_ge(xkv_used, CT * (n - 1) + c + 1)
                    act.activation(xs_hi[:, c, :], s_sb[:, 2 * t + c // 2, c % 2, :], ACT.Copy)\
                       .then_inc(xkv_hi, 1)

            def keys_values(t, n):
                u = t % 2
                if t == 0:
                    queries(n, q0_ps)
                act.wait_ge(xkv_used, CT * (n + 1))
                act.activation(k_hi[:, t * QC:(t + 1) * QC], s_ps[:, u, 0, :], ACT.Identity,
                               bias=bk_c[:, :]).then_inc(k_hi_done, 1)
                v_blocks = s_ps[:, u, 1, :].rearrange("p (a h c) -> p a h c", h=2, c=P)
                act.wait_ge(v_ready, n + 1)
                act.activation(v_hi[:, 2 * t:2 * t + 2, :], v_blocks[:, :, 1, :], ACT.Copy)\
                   .then_inc(v_hi_done, 1)
                act.activation(v_nat[:, 2 * t:2 * t + 2, :], v_blocks[:, :, 0, :], ACT.Copy)\
                   .then_inc(v_nat_done, 1)

            def split_x(c, m):
                act.wait_ge(xq_loaded, 16 * m)
                act.activation(xs_hi[:, c, :], x_raw[:, c, :], ACT.Copy).then_inc(xq_hi, 1)

            def queries(g, bank=q_ps):
                act.wait_ge(q_ready, START + g + 1)
                act.activation(q_hi[:, :], bank, ACT.Identity, bias=bq_c[:, :]).then_inc(q_hi_done, 1)

            def scores(p, g, over=None):
                act.wait_ge(s_ready, PAIRS * g + p + 1)
                if over is not None:
                    act.wait_ge(exps_done, PAIRS * over + p + 1)
                act.activation(s_sb[:, p, :, :], s_ps[:, p % 2, :, :], ACT.Copy).then_inc(s_saved, 1)

            def exp_whole(p, g):
                act.wait_ge(sub_done, PAIRS * g + p + 1)
                if p >= RING:
                    act.wait_ge(pv_done, PAIRS * g + p - RING + 1)
                    act.wait_ge(sum_done, PAIRS * g + p - RING + 1)
                act.activation(p_nat[:, p % RING, :], s_sb[:, p, 0, :], ACT.Exp).then_inc(expn_done, 1)

            def exp_split(p, g):
                act.activation(p_hi[:, p % RING, :], s_sb[:, p, 1, :], ACT.Exp)
                if p:
                    act.wait_ge(sum2_done, PAIRS * g + p)
                act.activation(p_ps[:, :], s_sb[:, p, 1, :], ACT.Exp).then_inc(exps_done, 1)

            def max_broadcast(g):
                act.wait_ge(maxb_ready, g + 1)
                act.activation(max_all[:, :], max_ps[:, :], ACT.Copy).then_inc(maxb_saved, 1)

            def second_layer(c, g):
                if g is not None:
                    act.wait_ge(y_ready, START + CT * g + c + 1)
                    act.activation(x_raw[:, c, :], y_ps[c], ACT.Gelu, bias=y_bias[:, c:c + 1])\
                       .then_inc(y_saved, 1)

            def between(y, maximum):
                second_layer(0, y)
                second_layer(1, y)
                second_layer(2, y)
                if maximum is not None:
                    max_broadcast(maximum)
                second_layer(3, y)

            def chunk(m, g, ahead, project, renew, y):
                for p in range(PAIRS):
                    exp_whole(p, g)
                    if ahead and p:
                        scores(p - 1, g + 1, over=g)
                    exp_split(p, g)
                    if project and SPLIT_AT <= p < SPLIT_AT + CT:
                        split_x(p - SPLIT_AT, m + 2)
                    for t in renewed_after(p) if renew is not None else ():
                        if t:
                            keys_values(t - 1, g + t)
                        split_x_kv(t, renew, g + 1 + t)
                if ahead:
                    scores(LAST, g + 1, over=g)
                if project:
                    queries(g + 2)
                if renew is not None:
                    for t in RENEWED_LAST:
                        keys_values(t - 1, g + t)
                        split_x_kv(t, renew, g + 1 + t)
                    keys_values(CHUNKS - 1, g + CHUNKS)
                between(g - 1 if y else None, g + 1 if ahead else None)

            def first_scores(m, g0, y):
                for p in range(PAIRS):
                    scores(p, g0)
                    if SPLIT_AT <= p < SPLIT_AT + CT:
                        split_x(p - SPLIT_AT, m + 1)
                queries(g0 + 1)
                between(y, g0)

            def image(b, last):
                g0 = b * CHUNKS
                m0 = b * (CHUNKS - 1)
                chunk(m0, g0, True, True, None, False)
                with act.Fori(1, CHUNKS - 2) as t:
                    chunk(m0 + t, g0 + t, True, True, None, True)
                chunk(m0 + CHUNKS - 2, g0 + CHUNKS - 2, True, False, None, True)
                chunk(m0 + CHUNKS - 1, g0 + CHUNKS - 1, False, False, None if last else b + 1, True)
                if not last:
                    first_scores(m0 + CHUNKS - 1, g0 + CHUNKS, g0 + CHUNKS - 1)
                else:
                    between(g0 + CHUNKS - 1, None)

            act.wait_ge(setup_saved, SETUP_STEPS)
            for t in range(CHUNKS):
                split_x_kv(t, 0, t)
                if t:
                    keys_values(t - 1, t - 1)
            keys_values(CHUNKS - 1, CHUNKS - 1)
            first_scores(0, 0, None)
            with act.Fori(0, B - 1) as b:
                image(b, False)
            image(B - 1, True)

        @block.gpsimd
        def _(pool):
            pool.memset(ones[:, :], 1.0).then_inc(consts_ready, 1)
            pool.memset(ident[:, :], 0.0).then_inc(ident_zero, 1)
            pool.wait_ge(ident_zero, 1)
            pool.affine_select(out=ident[:, :], in_=ident[:, :], compare_op=ALU.not_equal, fill=1.0,
                               base=0, pattern=[[-1, P]], channel_multiplier=1).then_inc(consts_ready, 1)

            def split_x(c, m):
                pool.wait_ge(xq_hi, CT * (m - 1) + c + 1)
                pool.tensor_tensor(xs_lo[:, c, :], x_raw[:, c, :], xs_hi[:, c, :].bitcast(fp32),
                                   ALU.subtract).then_inc(xq_lo, 1)

            def chunk(m, g, project):
                pool.wait_ge(maxb_saved, g + 1)
                for p in range(PAIRS):
                    pool.tensor_tensor(s_sb[:, p, :, :], s_sb[:, p, :, :],
                                       max_all[:, None, :].broadcast_to([P, 2, QC]), ALU.subtract)\
                        .then_inc(sub_done, 1)
                if project:
                    for c in range(CT):
                        split_x(c, m + 2)

            with pool.Fori(0, B) as b:
                g0 = b * CHUNKS
                m0 = b * (CHUNKS - 1)
                for c in range(CT):
                    split_x(c, m0 + 1)
                with pool.Fori(0, CHUNKS - 2) as t:
                    chunk(m0 + t, g0 + t, True)
                chunk(m0 + CHUNKS - 2, g0 + CHUNKS - 2, False)
                chunk(m0 + CHUNKS - 1, g0 + CHUNKS - 1, False)

        @block.vector
        def _(dve):
            dve.sem_inc(a_done, START)
            dve.wait_ge(consts_ready, 2)
            dve.wait_ge(w_loaded, 16 * LOADS)
            for g in range(CT):
                add = dve.tensor_tensor(M_sb[:, g, :], M_sb[:, g, :], ident[:, :], ALU.add)
            add.then_inc(m_ready, 1)
            for n in range(3):
                dve.wait_ge(setup_ps, n + 1)
                if n == 2:
                    dve.tensor_copy(wvT[:, :, :].rearrange("p c o -> p (c o)"), max_ps[:, :])\
                       .then_inc(setup_saved, 1)
                    continue
                hi = wT_hi[:, n, :, :].rearrange("p c o -> p (c o)")
                dve.tensor_copy(hi, max_ps[:, :]).then_inc(setup_hi, 1)
                dve.wait_ge(setup_hi, n + 1)
                dve.tensor_tensor(wT_lo[:, n, :, :].rearrange("p c o -> p (c o)"), max_ps[:, :],
                                  hi.bitcast(fp32), ALU.subtract).then_inc(setup_saved, 1)
            for g in range(CT):
                dve.wait_ge(setup_ps, 4 + g)
                dve.tensor_copy(woM[:, g, :], max_ps[:, 0:P]).then_inc(setup_saved, 1)
            dve.wait_ge(setup_ps, 4 + CT)
            dve.tensor_copy(y_bias[:, :], max_ps[:, 0:CT]).then_inc(setup_saved, 1)

            def split_x_kv(t, n):
                for c in range(CT):
                    dve.wait_ge(xkv_hi, CT * n + c + 1)
                    dve.tensor_tensor(xs_lo[:, c, :], s_sb[:, 2 * t + c // 2, c % 2, :],
                                      xs_hi[:, c, :].bitcast(fp32), ALU.subtract).then_inc(xkv_lo, 1)

            def keys_values(t, n):
                u = t % 2
                if t == 0:
                    queries(n, q0_ps)
                dve.wait_ge(k_hi_done, n + 1)
                cols = slice(t * QC, (t + 1) * QC)
                dve.scalar_tensor_tensor(out=k_lo[:, cols], in0=s_ps[:, u, 0, :], scalar=bk_c[:, :],
                                         in1=k_hi[:, cols].bitcast(fp32), op0=ALU.add,
                                         op1=ALU.subtract).then_inc(k_lo_done, 1)
                dve.wait_ge(v_hi_done, n + 1)
                dve.wait_ge(v_nat_done, n + 1)
                v_blocks = s_ps[:, u, 1, :].rearrange("p (a h c) -> p a h c", h=2, c=P)
                dve.tensor_tensor(v_lo[:, 2 * t:2 * t + 2, :], v_blocks[:, :, 1, :],
                                  v_hi[:, 2 * t:2 * t + 2, :].bitcast(fp32), ALU.subtract)\
                   .then_inc(v_lo_done, 1)

            def queries(g, bank=q_ps):
                dve.wait_ge(q_hi_done, g + 1)
                dve.scalar_tensor_tensor(out=q_lo[:, :], in0=bank, scalar=bq_c[:, :],
                                         in1=q_hi[:, :].bitcast(fp32), op0=ALU.add,
                                         op1=ALU.subtract).then_inc(q_lo_done, 1)

            def running_max(i, g):
                p, h = divmod(i, 2)
                if h == 0:
                    dve.wait_ge(s_saved, PAIRS * g + p + 1)
                tile = s_sb[:, p, h, :]
                if p == 0 and h == 0:
                    dve.tensor_copy(max_ps[:, :], tile).then_inc(max_done, 1)
                    return
                dve.wait_ge(max_done, 2 * (PAIRS * g + p) + h)
                to = max_sb if (p == LAST and h == 1) else max_ps
                dve.tensor_tensor(to[:, :], tile, max_ps[:, :], ALU.max).then_inc(max_done, 1)

            def sum_whole(p, g):
                dve.wait_ge(expn_done, PAIRS * g + p + 1)
                tile = p_nat[:, p % RING, :]
                if p == 0:
                    dve.tensor_copy(sum_ps[:, :], tile).then_inc(sum_done, 1)
                    return
                dve.wait_ge(sum_done, PAIRS * g + p)
                dve.tensor_tensor(sum_ps[:, :], tile, sum_ps[:, :], ALU.add).then_inc(sum_done, 1)

            def rest_of_split(p, g):
                dve.wait_ge(exps_done, PAIRS * g + p + 1)
                if p >= RING:
                    dve.wait_ge(pv_done, PAIRS * g + p - RING + 1)
                dve.tensor_tensor(p_lo[:, p % RING, :], p_ps[:, :], p_hi[:, p % RING, :].bitcast(fp32),
                                  ALU.subtract).then_inc(p_lo_done, 1)

            def sum_split(p, g):
                if p == 0:
                    dve.tensor_copy(sum2_sb[:, :], p_ps[:, :]).then_inc(sum2_done, 1)
                    return
                dve.wait_ge(sum2_done, PAIRS * g + p)
                dve.tensor_tensor(sum2_sb[:, :], p_ps[:, :], sum2_sb[:, :], ALU.add)\
                   .then_inc(sum2_done, 1)

            def total(g):
                dve.wait_ge(sum_done, PAIRS * (g + 1))
                dve.wait_ge(sum2_done, PAIRS * (g + 1))
                dve.tensor_tensor(sum_sb[:, :], sum_ps[:, :], sum2_sb[:, :], ALU.add)\
                   .then_inc(total_done, 1)

            def to_diagonal(column, diag, done):
                dve.tensor_tensor(diag[:, :, :], ident[:, None, :].broadcast_to([P, PT, P]),
                                  column[:, :, None].broadcast_to([P, PT, P]), ALU.mult)\
                   .then_inc(done, 1)

            def max_columns(g):
                dve.wait_ge(maxt_ready, g + 1)
                dve.tensor_reduce(max_col[:, :], max_t, AX.X, ALU.max).then_inc(maxcol_done, 1)
                dve.wait_ge(maxcol_done, g + 1)
                to_diagonal(max_col, max_diag, maxdiag_done)

            def normalise(g):
                dve.wait_ge(sumb_ready, g + 1)
                dve.reciprocal(rsum_all[:, :], sum_ps[:, :]).then_inc(rsum_done, 1)
                dve.wait_ge(rsum_done, g + 1)
                dve.wait_ge(y_ready, START + CT * g)
                dve.tensor_tensor(a_sb[:, :], pv_ps[:, :], rsum_all[:, :], ALU.mult).then_inc(a_done, 1)

            def chunk(g, ahead, project, renew, y):
                steps = 0
                for p in range(PAIRS):
                    until = min(2 * p, p * (2 * PAIRS - MAX_LAG) // LAST) if ahead else 0
                    sum_whole(p, g)
                    if steps < until:
                        running_max(steps, g + 1)
                        steps += 1
                    rest_of_split(p, g)
                    if steps < until:
                        running_max(steps, g + 1)
                        steps += 1
                    sum_split(p, g)
                    for t in renewed_after(p) if renew else ():
                        if t:
                            keys_values(t - 1, g + t)
                        split_x_kv(t, g + 1 + t)
                if renew:
                    for t in RENEWED_LAST:
                        keys_values(t - 1, g + t)
                        split_x_kv(t, g + 1 + t)
                    keys_values(CHUNKS - 1, g + CHUNKS)
                total(g)
                if ahead:
                    for i in range(steps, 2 * PAIRS):
                        running_max(i, g + 1)
                if project:
                    queries(g + 2)
                if ahead:
                    max_columns(g + 1)
                normalise(g)

            def first_scores(g0):
                for i in range(2 * PAIRS):
                    running_max(i, g0)
                queries(g0 + 1)
                max_columns(g0)

            def image(b, last):
                g0 = b * CHUNKS
                chunk(g0, True, True, False, False)
                with dve.Fori(1, CHUNKS - 2) as t:
                    chunk(g0 + t, True, True, False, True)
                chunk(g0 + CHUNKS - 2, True, False, False, True)
                chunk(g0 + CHUNKS - 1, False, False, not last, True)
                if not last:
                    first_scores(g0 + CHUNKS)

            for t in range(CHUNKS):
                split_x_kv(t, t)
                if t:
                    keys_values(t - 1, t - 1)
            keys_values(CHUNKS - 1, CHUNKS - 1)
            first_scores(0)
            with dve.Fori(0, B - 1) as b:
                image(b, False)
            image(B - 1, True)


_INS = ["x", "L0_conv_wq", "L0_conv_bq", "L0_conv_wk", "L0_conv_bk", "L0_conv_wv", "L0_conv_bv",
        "L0_conv_wo", "L0_conv_bo", "L1_conv_wc"]


def kernel(**inputs):
    import numpy as _np
    import concourse.bacc as _bacc
    from concourse import mybir as _mybir
    from concourse.bass_utils import run_bass_kernel_spmd as _run

    nc = _bacc.Bacc("TRN2", target_bir_lowering=False, num_devices=1)
    arrays, args = {}, []
    for name in _INS:
        a = _np.ascontiguousarray(inputs[name])
        arrays[f"in_{name}_dram"] = a
        args.append(nc.dram_tensor(f"in_{name}_dram", a.shape, _mybir.dt.from_np(a.dtype),
                                   kind="ExternalInput").ap())
    shape = tuple(inputs["x"].shape)
    out = nc.dram_tensor("out_dram", shape, _mybir.dt.float32, kind="ExternalOutput").ap()
    attention_conv_kernel(nc, *args, out)
    r = _run(nc, [arrays], core_ids=[0])
    return r.results[0]["out_dram"]
```

```python
import concourse.bass as bass
from concourse import mybir
from contextlib import ExitStack


def attention_conv_kernel(nc: bass.Bass, x: bass.AP, wq: bass.AP, bq: bass.AP, wk: bass.AP,
                          bk: bass.AP, wv: bass.AP, bv: bass.AP, wo: bass.AP, bo: bass.AP,
                          wc: bass.AP, out: bass.AP):
    fp32 = mybir.dt.float32
    fp32r = mybir.dt.float32r
    ALU = mybir.AluOpType
    ACT = mybir.ActivationFunctionType
    AX = mybir.AxisListType

    B, C, H, W = x.shape
    N = H * W
    P = 128
    CT = C // P
    QC = 512
    CHUNKS = N // QC
    PAIRS = N // P // 2
    PT = QC // P
    RING = 4
    SPLIT_AT = PAIRS // 2 - 2
    assert wq.shape[0] == P and wc.shape[1] == P and PAIRS == 2 * CHUNKS and CHUNKS > CT

    x_v = x.rearrange("b (c p) h w -> p b c (h w)", p=P)
    out_v = out.rearrange("b (c p) h w -> p b c (h w)", p=P)

    ctx = ExitStack()
    with ctx:
        def sb(name, shape, dt=fp32):
            return ctx.enter_context(nc.sbuf_tensor(name, shape, dt))

        def sem(name):
            return ctx.enter_context(nc.semaphore(name))

        wT_hi = sb("wT_hi", [P, 2, CT, P], fp32r)
        wT_lo = sb("wT_lo", [P, 2, CT, P], fp32r)
        wvT = sb("wvT", [P, CT, P])
        M_sb = sb("M_sb", [P, CT, P])
        woM_hi = sb("woM_hi", [P, CT, P], fp32r)
        woM_lo = sb("woM_lo", [P, CT, P], fp32r)
        bq_c = sb("bq_c", [P, 1])
        bk_c = sb("bk_c", [P, 1])
        bv_c = sb("bv_c", [P, 1])
        bo_c = sb("bo_c", [P, CT])
        y_bias = sb("y_bias", [P, CT])
        ident = sb("ident", [P, P])
        ones = sb("ones", [P, P])
        s_sb = sb("s_sb", [P, PAIRS, 2, QC])
        w_nat = s_sb[:, PAIRS - 2:PAIRS, :, :].rearrange("p a b n -> p (a b) n")
        wo_nat = w_nat[:, 3, :].rearrange("p (g c) -> p g c", g=CT)
        x_raw = sb("x_raw", [P, CT, QC])
        xs_hi = sb("xs_hi", [P, CT, QC], fp32r)
        xs_lo = sb("xs_lo", [P, CT, QC], fp32r)
        k_hi = sb("k_hi", [P, N], fp32r)
        k_lo = sb("k_lo", [P, N], fp32r)
        v_nat = sb("v_nat", [P, PAIRS, P])
        v_hi = sb("v_hi", [P, PAIRS, P], fp32r)
        v_lo = sb("v_lo", [P, PAIRS, P], fp32r)
        q_hi = sb("q_hi", [P, QC], fp32r)
        q_lo = sb("q_lo", [P, QC], fp32r)
        p_nat = sb("p_nat", [P, RING, QC])
        p_hi = sb("p_hi", [P, RING, QC], fp32r)
        p_lo = sb("p_lo", [P, RING, QC], fp32r)
        max_sb = sb("max_sb", [P, QC])
        max_col = sb("max_col", [P, PT])
        max_all = sb("max_all", [P, QC])
        sum_sb = sb("sum_sb", [P, QC])
        rsum_all = sb("rsum_all", [P, QC])
        max_diag = sb("max_diag", [P, PT, P])
        a_hi = sb("a_hi", [P, QC], fp32r)
        a_lo = sb("a_lo", [P, QC], fp32r)

        def bank(name, shape):
            return ctx.enter_context(nc.psum_tensor(name, shape, fp32))

        s_ps = bank("s_ps", [P, 2, 2, QC])
        pv_ps = bank("pv_ps", [P, QC])
        p_ps = bank("p_ps", [P, QC])
        sum_ps = bank("sum_ps", [P, QC])
        max_ps = bank("max_ps", [P, QC])
        q_ps = s_ps[:, 0, 0, :]
        q0_ps = s_ps[:, 1, 0, :]
        y_ps = [s_ps[:, 0, 1, :], s_ps[:, 1, 0, :], s_ps[:, 0, 0, :], s_ps[:, 1, 1, :]]
        max_t = max_ps[:, :].rearrange("p (k j) -> p k j", k=PT)

        wqkv_loaded = sem("wqkv_loaded")
        b_loaded = sem("b_loaded")
        w2_loaded = sem("w2_loaded")
        consts_ready = sem("consts_ready")
        ident_zero = sem("ident_zero")
        m_ready = sem("m_ready")
        setup_ps = sem("setup_ps")
        setup_hi = sem("setup_hi")
        setup_saved = sem("setup_saved")
        xkv_loaded = [sem(f"xkv_loaded{t}") for t in range(CHUNKS)]
        xq_loaded = sem("xq_loaded")
        xy_loaded = sem("xy_loaded")
        y_stored = sem("y_stored")
        xkv_hi = sem("xkv_hi")
        xkv_lo = sem("xkv_lo")
        xkv_used = sem("xkv_used")
        k_hi_done = sem("k_hi_done")
        k_lo_done = sem("k_lo_done")
        v_ready = sem("v_ready")
        v_hi_done = sem("v_hi_done")
        v_lo_done = sem("v_lo_done")
        v_nat_done = sem("v_nat_done")
        xq_hi = sem("xq_hi")
        xq_lo = sem("xq_lo")
        q_ready = sem("q_ready")
        q_hi_done = sem("q_hi_done")
        q_lo_done = sem("q_lo_done")
        s_ready = sem("s_ready")
        s_saved = sem("s_saved")
        max_done = sem("max_done")
        maxt_ready = sem("maxt_ready")
        maxcol_done = sem("maxcol_done")
        maxdiag_done = sem("maxdiag_done")
        maxb_ready = sem("maxb_ready")
        maxb_saved = sem("maxb_saved")
        first_sub_done = sem("first_sub_done")
        sub_done = sem("sub_done")
        expn_done = sem("expn_done")
        exps_done = sem("exps_done")
        p_lo_done = sem("p_lo_done")
        pv_done = sem("pv_done")
        sum_done = sem("sum_done")
        sum2_done = sem("sum2_done")
        total_done = sem("total_done")
        sumb_ready = sem("sumb_ready")
        rsum_done = sem("rsum_done")
        a_done = sem("a_done")
        a_hi_done = sem("a_hi_done")
        a_lo_done = sem("a_lo_done")
        y_ready = sem("y_ready")
        y_saved = sem("y_saved")

        SETUP_STEPS = 3 + CT + 1
        LOADS2 = 2 + CT
        LAST = PAIRS - 1
        MAX_STEPS = 2 * PAIRS - 1
        MAX_LAG = 5
        POOL_SPLIT_AT = LAST - CT
        SPLIT_A_AT = 6

        def renewed_after(p):
            t = (p - 1 - RENEW_LAG) // 2
            return [t] if t >= 0 and (p - 1 - RENEW_LAG) % 2 == 0 else []

        RENEW_LAG = 2
        RENEWED_LAST = [t for t in range(CHUNKS) if 2 * t + 1 + RENEW_LAG > LAST]
        START = CT
        block = ctx.enter_context(nc.Block())


        @block.sync
        def _(sp):
            sp.sem_inc(y_stored, START)
            for n, w in enumerate((wq, wk, wv)):
                sp.dma_start(w_nat[:, n, :], w).then_inc(wqkv_loaded, 16)

            def x_chunk(b, t):
                return x_v[:, bass.ds(b, 1), :, bass.ds(t * QC, QC)].rearrange("p a c n -> p (a c) n")

            def load_kv(b, n):
                sp.dma_start(s_sb[:, 2 * n:2 * n + 2, :, :].rearrange("p a b n -> p (a b) n"),
                             x_chunk(b, n)).then_inc(xkv_loaded[n], 16)

            def load_q(b, t):
                sp.dma_start(x_raw[:, :, :], x_chunk(b, t)).then_inc(xq_loaded, 16)

            def load_y(b, t):
                sp.dma_start(x_raw[:, :, :], x_chunk(b, t)).then_inc(xy_loaded, 16)

            def store(b, t, g):
                sp.wait_ge(y_saved, START + CT * (g + 1))
                sp.dma_start(out_v[:, bass.ds(b, 1), :, bass.ds(t * QC, QC)]
                             .rearrange("p a c n -> p (a c) n"), x_raw[:, :, :]).then_inc(y_stored, 16)

            def image(b, last):
                g0 = b * CHUNKS
                m0 = b * (CHUNKS - 1)
                sp.wait_ge(xq_lo, CT * (m0 + 1))
                sp.wait_ge(y_stored, START + 16 * g0)
                load_q(b, 2)
                with sp.Fori(1, CHUNKS - 2) as t:
                    g = g0 + t
                    sp.wait_ge(xq_lo, CT * (m0 + t + 1))
                    sp.wait_ge(y_stored, START + 16 * (g - 1))
                    load_q(b, t + 2)
                    sp.wait_ge(xq_lo, CT * (m0 + t + 2))
                    load_y(b, t - 1)
                    store(b, t - 1, g - 1)
                for t in range(CHUNKS - 2, CHUNKS):
                    g = g0 + t
                    sp.wait_ge(y_stored, START + 16 * (g - 1))
                    load_y(b, t - 1)
                    if t == CHUNKS - 1 and not last:
                        for n in range(CHUNKS):
                            sp.wait_ge(exps_done, PAIRS * g + 2 * n + 2)
                            load_kv(b + 1, n)
                    store(b, t - 1, g - 1)
                g = g0 + CHUNKS - 1
                sp.wait_ge(y_stored, START + 16 * g)
                if not last:
                    load_q(b + 1, 1)
                    sp.wait_ge(xq_lo, CT * (m0 + CHUNKS))
                load_y(b, CHUNKS - 1)
                store(b, CHUNKS - 1, g)

            load_kv(0, 0)
            for column, bias in ((bq_c, bq), (bk_c, bk), (bv_c, bv)):
                sp.dma_start(column[:, :], bias.rearrange("(p a) -> p a", a=1)).then_inc(b_loaded, 16)
            load_kv(0, 1)
            sp.dma_start(wo_nat, wo.rearrange("(g p) c -> p g c", p=P)).then_inc(w2_loaded, 16)
            sp.dma_start(M_sb[:, :, :], wc.rearrange("g j k -> j g k")).then_inc(w2_loaded, 16)
            for g in range(CT):
                sp.dma_start(bo_c[:, g:g + 1], bo[g * P:(g + 1) * P].rearrange("(p a) -> p a", a=1))\
                  .then_inc(w2_loaded, 16)
            for n in range(2, CHUNKS):
                if n == CHUNKS - 1:
                    sp.wait_ge(setup_saved, SETUP_STEPS)
                load_kv(0, n)
            load_q(0, 1)
            with sp.Fori(0, B - 1) as b:
                image(b, False)
            image(B - 1, True)
            sp.wait_ge(y_stored, START + 16 * B * CHUNKS)

        @block.tensor
        def _(pe):
            pe.sem_inc(q_ready, START)
            pe.sem_inc(pv_done, START)
            pe.wait_ge(wqkv_loaded, 16 * 3)
            pe.wait_ge(consts_ready, 2)
            for n in range(3):
                if n:
                    pe.wait_ge(setup_saved, n)
                for c in range(CT):
                    mm = pe.transpose(max_ps[:, c * P:(c + 1) * P], w_nat[:, n, c * P:(c + 1) * P],
                                      ident[:, :])
                mm.then_inc(setup_ps, 1)
            pe.wait_ge(setup_saved, 3)

            def second_weights(t):
                if t > CT:
                    return
                pe.wait_ge(m_ready, 1)
                pe.wait_ge(setup_saved, 3 + t)
                if t < CT:
                    pe.matmul(max_ps[:, 0:P], wo_nat[:, t, :], M_sb[:, t, :], start=True, stop=True)\
                      .then_inc(setup_ps, 1)
                    return
                pe.wait_ge(b_loaded, 16 * 3)
                for g in range(CT):
                    pe.matmul(max_ps[:, g:g + 1], woM_lo[:, g, :].bitcast(fp32), bv_c[:, :],
                              start=True, stop=False)
                    pe.matmul(max_ps[:, g:g + 1], woM_hi[:, g, :].bitcast(fp32), bv_c[:, :],
                              start=False, stop=False)
                    mm = pe.matmul(max_ps[:, g:g + 1], M_sb[:, g, :], bo_c[:, g:g + 1],
                                   start=False, stop=True)
                mm.then_inc(setup_ps, 1)

            def split_product(o, a_lo, a_hi, b_lo, b_hi, start, stop, **more):
                pe.matmul(o, a_lo, b_hi, start=start, stop=False, **more)
                pe.matmul(o, a_hi, b_lo, start=False, stop=False, **more)
                return pe.matmul(o, a_hi, b_hi, start=False, stop=stop, **more)

            def keys_values(t, n):
                u = t % 2
                if t >= 2:
                    pe.wait_ge(k_lo_done, n - 1)
                    pe.wait_ge(v_lo_done, n - 1)
                if t == 0:
                    for c in range(CT):
                        pe.wait_ge(xkv_lo, CT * n + c + 1)
                        mm = split_product(q0_ps, wT_lo[:, 0, c, :], wT_hi[:, 0, c, :], xs_lo[:, c, :],
                                           xs_hi[:, c, :], start=(c == 0), stop=(c == CT - 1))
                    mm.then_inc(q_ready, 1)
                if t == 1:
                    pe.wait_ge(q_lo_done, n)
                for c in range(CT):
                    pe.wait_ge(xkv_lo, CT * n + c + 1)
                    split_product(s_ps[:, u, 0, :], wT_lo[:, 1, c, :], wT_hi[:, 1, c, :], xs_lo[:, c, :],
                                  xs_hi[:, c, :], start=(c == 0), stop=(c == CT - 1))\
                        .then_inc(xkv_used, 1)
                for k in range(PT):
                    for c in range(CT):
                        mm = pe.matmul(s_ps[:, u, 1, k * P:(k + 1) * P],
                                       s_sb[:, 2 * t + c // 2, c % 2, k * P:(k + 1) * P],
                                       wvT[:, c, :], start=(c == 0), stop=(c == CT - 1))
                mm.then_inc(v_ready, 1)

            def queries(m, g):
                for c in range(CT):
                    pe.wait_ge(xq_lo, CT * (m - 1) + c + 1)
                    mm = split_product(q_ps, wT_lo[:, 0, c, :], wT_hi[:, 0, c, :], xs_lo[:, c, :],
                                       xs_hi[:, c, :], start=(c == 0), stop=(c == CT - 1))
                mm.then_inc(q_ready, 1)

            def scores(p, g):
                if p >= 2:
                    pe.wait_ge(s_saved, PAIRS * g + p - 1)
                for h in range(2):
                    keys = slice((2 * p + h) * P, (2 * p + h + 1) * P)
                    mm = split_product(s_ps[:, p % 2, h, :], k_lo[:, keys], k_hi[:, keys],
                                       q_lo[:, :], q_hi[:, :], start=True, stop=True)
                mm.then_inc(s_ready, 1)

            def values(p, g):
                r = p % RING
                pe.wait_ge(expn_done, PAIRS * g + p + 1)
                pe.matmul(pv_ps[:, :], v_nat[:, p, :], p_nat[:, r, :], start=(p == 0), stop=False)
                pe.wait_ge(p_lo_done, PAIRS * g + p + 1)
                split_product(pv_ps[:, :], v_lo[:, p, :], v_hi[:, p, :], p_lo[:, r, :], p_hi[:, r, :],
                              start=False, stop=(p == LAST)).then_inc(pv_done, 1)

            def max_transpose(g):
                pe.wait_ge(max_done, MAX_STEPS * (g + 1))
                for k in range(PT):
                    mm = pe.transpose(max_t[:, k, :], max_sb[:, k * P:(k + 1) * P], ident[:, :])
                mm.then_inc(maxt_ready, 1)

            def max_broadcast(g):
                pe.wait_ge(maxdiag_done, g + 1)
                pe.matmul(max_ps[:, :], ones[:, :], max_diag[:, :, :].rearrange("p k j -> p (k j)"),
                          start=True, stop=True)\
                  .then_inc(maxb_ready, 1)

            def sum_broadcast(g):
                pe.wait_ge(total_done, g + 1)
                pe.matmul(sum_ps[:, :], ones[:, :], sum_sb[:, :], start=True, stop=True)\
                  .then_inc(sumb_ready, 1)

            def second_layer(c, g):
                if g is not None:
                    if c == 0:
                        pe.wait_ge(xy_loaded, 16 * (g + 1))
                    pe.matmul(y_ps[c], M_sb[:, c, :], x_raw[:, c, :], start=True, stop=False)
                    if c == 0:
                        pe.wait_ge(a_lo_done, START + g + 1)
                    split_product(y_ps[c], woM_lo[:, c, :], woM_hi[:, c, :], a_lo[:, :], a_hi[:, :],
                                  start=False, stop=True).then_inc(y_ready, 1)

            def between(y, maximum, total, projected, late):
                second_layer(0, y)
                if maximum is not None:
                    pe.wait_ge(s_saved, PAIRS * (maximum + 1))
                second_layer(1, y)
                if projected:
                    pe.wait_ge(q_lo_done, maximum + 2)
                second_layer(2, y)
                if maximum is not None:
                    max_transpose(maximum)
                second_layer(3, y)
                if maximum is not None:
                    max_broadcast(maximum)
                if total is not None:
                    sum_broadcast(total)
                if late:
                    values(LAST, total)

            def chunk(m, g, ahead, project, renew, y):
                if ahead:
                    pe.wait_ge(q_lo_done, g + 2)
                if renew:
                    pe.wait_ge(y_saved, START + CT * (g - 1))
                for p in range(PAIRS):
                    if ahead:
                        if p < 2:
                            pe.wait_ge(y_saved, START + CT * (g - 1 if y else g) - (1 - p))
                        scores(p, g + 1)
                    if p == 1:
                        pe.wait_ge(a_done, START + g)
                    if p:
                        values(p - 1, g)
                        for t in renewed_after(p - 1) if renew else ():
                            keys_values(t, g + 1 + t)
                if ahead or project:
                    pe.wait_ge(s_saved, PAIRS * (g + 2) - 1)
                if project:
                    queries(m + 2, g + 2)
                late = ahead and project and y
                if not late:
                    values(LAST, g)
                if renew:
                    for t in renewed_after(LAST) + RENEWED_LAST:
                        keys_values(t, g + 1 + t)
                    pe.wait_ge(k_lo_done, g + 1 + CHUNKS)
                    pe.wait_ge(v_lo_done, g + 1 + CHUNKS)
                between(g - 1 if y else None, g + 1 if ahead else None, g, project, late)

            def first_scores(m, g0, y):
                pe.wait_ge(q_lo_done, g0 + 1)
                for p in range(PAIRS):
                    scores(p, g0)
                pe.wait_ge(s_saved, PAIRS * (g0 + 1) - 1)
                queries(m + 1, g0 + 1)
                between(y, g0, None, True, False)

            def image(b, last):
                g0 = b * CHUNKS
                m0 = b * (CHUNKS - 1)
                chunk(m0, g0, True, True, False, False)
                with pe.Fori(1, CHUNKS - 2) as t:
                    chunk(m0 + t, g0 + t, True, True, False, True)
                chunk(m0 + CHUNKS - 2, g0 + CHUNKS - 2, True, False, False, True)
                chunk(m0 + CHUNKS - 1, g0 + CHUNKS - 1, False, False, not last, True)
                pe.wait_ge(y_saved, START + CT * (g0 + CHUNKS - 1))
                if not last:
                    first_scores(m0 + CHUNKS - 1, g0 + CHUNKS, g0 + CHUNKS - 1)
                else:
                    between(g0 + CHUNKS - 1, None, None, False, False)

            for t in range(CHUNKS):
                keys_values(t, t)
                second_weights(t)
            pe.wait_ge(setup_saved, SETUP_STEPS)
            pe.wait_ge(k_lo_done, CHUNKS)
            pe.wait_ge(v_lo_done, CHUNKS)
            first_scores(0, 0, None)
            with pe.Fori(0, B - 1) as b:
                image(b, False)
            image(B - 1, True)

        @block.scalar
        def _(act):
            act.sem_inc(y_saved, START)

            def split_x_kv(t, image, n):
                act.wait_ge(xkv_loaded[t], 16 * (image + 1))
                for c in range(CT):
                    if t:
                        act.wait_ge(xkv_used, CT * (n - 1) + c + 1)
                    act.activation(xs_hi[:, c, :], s_sb[:, 2 * t + c // 2, c % 2, :], ACT.Copy)\
                       .then_inc(xkv_hi, 1)

            def keys(t, n):
                u = t % 2
                if t == 0:
                    queries(n, q0_ps)
                act.wait_ge(xkv_used, CT * (n + 1))
                act.activation(k_hi[:, t * QC:(t + 1) * QC], s_ps[:, u, 0, :], ACT.Identity,
                               bias=bk_c[:, :]).then_inc(k_hi_done, 1)

            def values(t, n):
                v_blocks = s_ps[:, t % 2, 1, :].rearrange("p (a h c) -> p a h c", h=2, c=P)
                act.wait_ge(v_ready, n + 1)
                act.activation(v_hi[:, 2 * t:2 * t + 2, :], v_blocks[:, :, 1, :], ACT.Copy)\
                   .then_inc(v_hi_done, 1)
                act.activation(v_nat[:, 2 * t:2 * t + 2, :], v_blocks[:, :, 0, :], ACT.Copy)\
                   .then_inc(v_nat_done, 1)

            def renew_step(t, image, n):
                if t:
                    keys(t - 1, n - 1)
                if t < CHUNKS:
                    split_x_kv(t, image, n)
                if t:
                    values(t - 1, n - 1)

            def split_x(c, m):
                act.wait_ge(xq_loaded, 16 * m)
                act.activation(xs_hi[:, c, :], x_raw[:, c, :], ACT.Copy).then_inc(xq_hi, 1)

            def queries(g, bank=q_ps):
                act.wait_ge(q_ready, START + g + 1)
                act.activation(q_hi[:, :], bank, ACT.Identity, bias=bq_c[:, :]).then_inc(q_hi_done, 1)

            def scores(p, g, over=None):
                act.wait_ge(s_ready, PAIRS * g + p + 1)
                if over is not None:
                    act.wait_ge(exps_done, PAIRS * over + p + 1)
                act.activation(s_sb[:, p, :, :], s_ps[:, p % 2, :, :], ACT.Copy).then_inc(s_saved, 1)

            def exp_whole(p, g):
                if p == 0:
                    act.wait_ge(first_sub_done, g + 1)
                else:
                    act.wait_ge(sub_done, PAIRS * g + p + 1)
                if p >= RING - 1:
                    act.wait_ge(pv_done, START + PAIRS * g + p - RING + 1)
                    if p > RING:
                        act.wait_ge(sum_done, LAST * g + p - RING)
                act.activation(p_nat[:, p % RING, :], s_sb[:, p, 0, :], ACT.Exp).then_inc(expn_done, 1)

            def exp_split(p, g):
                if p == 0:
                    act.wait_ge(sub_done, PAIRS * g + 1)
                act.activation(p_hi[:, p % RING, :], s_sb[:, p, 1, :], ACT.Exp)
                if p:
                    act.wait_ge(sum2_done, PAIRS * g + p)
                act.activation(p_ps[:, :], s_sb[:, p, 1, :], ACT.Exp).then_inc(exps_done, 1)

            def max_broadcast(g):
                act.wait_ge(maxb_ready, g + 1)
                act.activation(max_all[:, :], max_ps[:, :], ACT.Copy).then_inc(maxb_saved, 1)

            def second_layer(c, g):
                if g is not None:
                    act.wait_ge(y_ready, CT * g + c + 1)
                    act.activation(x_raw[:, c, :], y_ps[c], ACT.Gelu, bias=y_bias[:, c:c + 1])\
                       .then_inc(y_saved, 1)

            def split_a(g):
                act.wait_ge(a_done, START + g + 1)
                act.activation(a_hi[:, :], rsum_all[:, :], ACT.Copy).then_inc(a_hi_done, 1)

            def between(y, maximum):
                second_layer(0, y)
                second_layer(1, y)
                second_layer(2, y)
                second_layer(3, y)
                if maximum is not None:
                    max_broadcast(maximum)

            def chunk(m, g, ahead, project, renew, y):
                for p in range(PAIRS):
                    exp_whole(p, g)
                    if ahead and p:
                        scores(p - 1, g + 1, over=g)
                    if p == SPLIT_A_AT and y:
                        split_a(g - 1)
                    exp_split(p, g)
                    if project and SPLIT_AT <= p < SPLIT_AT + CT:
                        split_x(p - SPLIT_AT, m + 2)
                    for t in renewed_after(p) if renew is not None else ():
                        renew_step(t, renew, g + 1 + t)
                if ahead:
                    scores(LAST, g + 1, over=g)
                if project:
                    queries(g + 2)
                if renew is not None:
                    for t in RENEWED_LAST:
                        renew_step(t, renew, g + 1 + t)
                    renew_step(CHUNKS, renew, g + 1 + CHUNKS)
                between(g - 1 if y else None, g + 1 if ahead else None)

            def first_scores(m, g0, y):
                for p in range(PAIRS):
                    scores(p, g0)
                    if p == SPLIT_A_AT and y is not None:
                        split_a(y)
                    if SPLIT_AT <= p < SPLIT_AT + CT:
                        split_x(p - SPLIT_AT, m + 1)
                queries(g0 + 1)
                between(y, g0)

            def image(b, last):
                g0 = b * CHUNKS
                m0 = b * (CHUNKS - 1)
                chunk(m0, g0, True, True, None, False)
                with act.Fori(1, CHUNKS - 2) as t:
                    chunk(m0 + t, g0 + t, True, True, None, True)
                chunk(m0 + CHUNKS - 2, g0 + CHUNKS - 2, True, False, None, True)
                chunk(m0 + CHUNKS - 1, g0 + CHUNKS - 1, False, False, None if last else b + 1, True)
                if not last:
                    first_scores(m0 + CHUNKS - 1, g0 + CHUNKS, g0 + CHUNKS - 1)
                else:
                    split_a(g0 + CHUNKS - 1)
                    between(g0 + CHUNKS - 1, None)

            act.wait_ge(b_loaded, 16 * 3)
            for t in range(CHUNKS):
                renew_step(t, 0, t)
            renew_step(CHUNKS, 0, CHUNKS)
            act.wait_ge(setup_saved, SETUP_STEPS)
            first_scores(0, 0, None)
            with act.Fori(0, B - 1) as b:
                image(b, False)
            image(B - 1, True)

        @block.gpsimd
        def _(pool):
            pool.sem_inc(a_lo_done, START)
            pool.memset(ones[:, :], 1.0).then_inc(consts_ready, 1)
            pool.memset(ident[:, :], 0.0).then_inc(ident_zero, 1)
            pool.wait_ge(ident_zero, 1)
            pool.affine_select(out=ident[:, :], in_=ident[:, :], compare_op=ALU.not_equal, fill=1.0,
                               base=0, pattern=[[-1, P]], channel_multiplier=1).then_inc(consts_ready, 1)

            def split_x(c, m):
                pool.wait_ge(xq_hi, CT * (m - 1) + c + 1)
                pool.tensor_tensor(xs_lo[:, c, :], x_raw[:, c, :], xs_hi[:, c, :].bitcast(fp32),
                                   ALU.subtract).then_inc(xq_lo, 1)

            def split_a(g):
                pool.wait_ge(a_hi_done, g + 1)
                pool.tensor_tensor(a_lo[:, :], rsum_all[:, :], a_hi[:, :].bitcast(fp32),
                                   ALU.subtract).then_inc(a_lo_done, 1)

            def chunk(m, g, project, y=True):
                pool.wait_ge(maxb_saved, g + 1)
                for p in range(PAIRS):
                    if p == SPLIT_A_AT + 2 and y:
                        split_a(g - 1)
                    if p == 0:
                        for h, done in ((0, first_sub_done), (1, sub_done)):
                            pool.tensor_tensor(s_sb[:, 0, h, :], s_sb[:, 0, h, :], max_all[:, :],
                                               ALU.subtract).then_inc(done, 1)
                        continue
                    pool.tensor_tensor(s_sb[:, p, :, :], s_sb[:, p, :, :],
                                       max_all[:, None, :].broadcast_to([P, 2, QC]), ALU.subtract)\
                        .then_inc(sub_done, 1)
                    if project and POOL_SPLIT_AT <= p < POOL_SPLIT_AT + CT:
                        split_x(p - POOL_SPLIT_AT, m + 2)

            with pool.Fori(0, B) as b:
                g0 = b * CHUNKS
                m0 = b * (CHUNKS - 1)
                for c in range(CT):
                    split_x(c, m0 + 1)
                chunk(m0, g0, True, False)
                with pool.Fori(1, CHUNKS - 2) as t:
                    chunk(m0 + t, g0 + t, True)
                chunk(m0 + CHUNKS - 2, g0 + CHUNKS - 2, False)
                chunk(m0 + CHUNKS - 1, g0 + CHUNKS - 1, False)
                split_a(g0 + CHUNKS - 1)

        @block.vector
        def _(dve):
            dve.sem_inc(a_done, START)
            dve.wait_ge(consts_ready, 2)
            for n in range(3):
                dve.wait_ge(setup_ps, n + 1)
                if n == 2:
                    dve.tensor_copy(wvT[:, :, :].rearrange("p c o -> p (c o)"), max_ps[:, :])\
                       .then_inc(setup_saved, 1)
                    continue
                hi = wT_hi[:, n, :, :].rearrange("p c o -> p (c o)")
                dve.tensor_copy(hi, max_ps[:, :]).then_inc(setup_hi, 1)
                dve.wait_ge(setup_hi, n + 1)
                dve.tensor_tensor(wT_lo[:, n, :, :].rearrange("p c o -> p (c o)"), max_ps[:, :],
                                  hi.bitcast(fp32), ALU.subtract).then_inc(setup_saved, 1)
            dve.wait_ge(b_loaded, 16 * 3)

            def second_weights(t):
                if t == 0:
                    dve.wait_ge(w2_loaded, 16 * LOADS2)
                    for g in range(CT):
                        add = dve.tensor_tensor(M_sb[:, g, :], M_sb[:, g, :], ident[:, :], ALU.add)
                    add.then_inc(m_ready, 1)
                if t > CT:
                    return
                dve.wait_ge(setup_ps, 4 + t)
                if t == CT:
                    dve.tensor_copy(y_bias[:, :], max_ps[:, 0:CT]).then_inc(setup_saved, 1)
                    return
                dve.tensor_copy(woM_hi[:, t, :], max_ps[:, 0:P]).then_inc(setup_hi, 1)
                dve.wait_ge(setup_hi, 3 + t)
                dve.tensor_tensor(woM_lo[:, t, :], max_ps[:, 0:P], woM_hi[:, t, :].bitcast(fp32),
                                  ALU.subtract).then_inc(setup_saved, 1)

            def split_x_kv(t, n):
                for c in range(CT):
                    dve.wait_ge(xkv_hi, CT * n + c + 1)
                    dve.tensor_tensor(xs_lo[:, c, :], s_sb[:, 2 * t + c // 2, c % 2, :],
                                      xs_hi[:, c, :].bitcast(fp32), ALU.subtract).then_inc(xkv_lo, 1)

            def keys(t, n):
                u = t % 2
                if t == 0:
                    queries(n, q0_ps)
                dve.wait_ge(k_hi_done, n + 1)
                cols = slice(t * QC, (t + 1) * QC)
                dve.scalar_tensor_tensor(out=k_lo[:, cols], in0=s_ps[:, u, 0, :], scalar=bk_c[:, :],
                                         in1=k_hi[:, cols].bitcast(fp32), op0=ALU.add,
                                         op1=ALU.subtract).then_inc(k_lo_done, 1)

            def values(t, n):
                dve.wait_ge(v_hi_done, n + 1)
                dve.wait_ge(v_nat_done, n + 1)
                v_blocks = s_ps[:, t % 2, 1, :].rearrange("p (a h c) -> p a h c", h=2, c=P)
                dve.tensor_tensor(v_lo[:, 2 * t:2 * t + 2, :], v_blocks[:, :, 1, :],
                                  v_hi[:, 2 * t:2 * t + 2, :].bitcast(fp32), ALU.subtract)\
                   .then_inc(v_lo_done, 1)

            def renew_step(t, n):
                if t:
                    keys(t - 1, n - 1)
                if t < CHUNKS:
                    split_x_kv(t, n)
                if t:
                    values(t - 1, n - 1)

            def queries(g, bank=q_ps):
                dve.wait_ge(q_hi_done, g + 1)
                dve.scalar_tensor_tensor(out=q_lo[:, :], in0=bank, scalar=bq_c[:, :],
                                         in1=q_hi[:, :].bitcast(fp32), op0=ALU.add,
                                         op1=ALU.subtract).then_inc(q_lo_done, 1)

            def running_max(i, g):
                p, h = divmod(i + 1, 2)
                if h == 0 or i == 0:
                    dve.wait_ge(s_saved, PAIRS * g + p + 1)
                if i:
                    dve.wait_ge(max_done, MAX_STEPS * g + i)
                before = max_ps[:, :] if i else s_sb[:, 0, 0, :]
                to = max_sb if i == MAX_STEPS - 1 else max_ps
                dve.tensor_tensor(to[:, :], s_sb[:, p, h, :], before, ALU.max).then_inc(max_done, 1)

            def sum_whole(p, g):
                dve.wait_ge(expn_done, PAIRS * g + p + 1)
                tile = p_nat[:, p % RING, :]
                if p == 1:
                    dve.tensor_copy(sum_ps[:, :], tile).then_inc(sum_done, 1)
                else:
                    dve.wait_ge(sum_done, LAST * g + p - 1)
                    dve.tensor_tensor(sum_ps[:, :], tile, sum_ps[:, :], ALU.add).then_inc(sum_done, 1)

            def rest_of_split(p, g):
                dve.wait_ge(exps_done, PAIRS * g + p + 1)
                if p >= RING - 1:
                    dve.wait_ge(pv_done, START + PAIRS * g + p - RING + 1)
                dve.tensor_tensor(p_lo[:, p % RING, :], p_ps[:, :], p_hi[:, p % RING, :].bitcast(fp32),
                                  ALU.subtract).then_inc(p_lo_done, 1)

            def sum_split(p, g):
                if p:
                    dve.wait_ge(sum2_done, PAIRS * g + p)
                before = sum_sb[:, :] if p else p_nat[:, 0, :]
                dve.tensor_tensor(sum_sb[:, :], p_ps[:, :], before, ALU.add).then_inc(sum2_done, 1)

            def total(g):
                dve.wait_ge(sum_done, LAST * (g + 1))
                dve.wait_ge(sum2_done, PAIRS * (g + 1))
                dve.tensor_tensor(sum_sb[:, :], sum_ps[:, :], sum_sb[:, :], ALU.add)\
                   .then_inc(total_done, 1)

            def to_diagonal(column, diag, done):
                dve.tensor_tensor(diag[:, :, :], ident[:, None, :].broadcast_to([P, PT, P]),
                                  column[:, :, None].broadcast_to([P, PT, P]), ALU.mult)\
                   .then_inc(done, 1)

            def max_columns(g):
                dve.wait_ge(maxt_ready, g + 1)
                dve.tensor_reduce(max_col[:, :], max_t, AX.X, ALU.max).then_inc(maxcol_done, 1)
                dve.wait_ge(maxcol_done, g + 1)
                to_diagonal(max_col, max_diag, maxdiag_done)

            def normalise(g):
                dve.wait_ge(sumb_ready, g + 1)
                dve.wait_ge(a_lo_done, START + g)
                dve.reciprocal(rsum_all[:, :], sum_ps[:, :]).then_inc(rsum_done, 1)
                dve.wait_ge(rsum_done, g + 1)
                dve.wait_ge(pv_done, START + PAIRS * (g + 1))
                dve.tensor_tensor(rsum_all[:, :], pv_ps[:, :], rsum_all[:, :], ALU.mult)\
                   .then_inc(a_done, 1)

            def chunk(g, ahead, project, renew):
                steps = 0
                for p in range(PAIRS):
                    until = min(2 * p - 1, p * (MAX_STEPS - MAX_LAG) // LAST) if ahead else 0
                    if p:
                        sum_whole(p, g)
                    if steps < until:
                        running_max(steps, g + 1)
                        steps += 1
                    rest_of_split(p, g)
                    if steps < until:
                        running_max(steps, g + 1)
                        steps += 1
                    sum_split(p, g)
                    for t in renewed_after(p) if renew else ():
                        renew_step(t, g + 1 + t)
                if renew:
                    for t in RENEWED_LAST:
                        renew_step(t, g + 1 + t)
                    renew_step(CHUNKS, g + 1 + CHUNKS)
                if ahead:
                    for i in range(steps, MAX_STEPS):
                        if project and i == MAX_STEPS - 3:
                            queries(g + 2)
                        running_max(i, g + 1)
                total(g)
                if ahead:
                    max_columns(g + 1)
                normalise(g)

            def first_scores(g0):
                for i in range(MAX_STEPS):
                    running_max(i, g0)
                queries(g0 + 1)
                max_columns(g0)

            def image(b, last):
                g0 = b * CHUNKS
                chunk(g0, True, True, False)
                with dve.Fori(1, CHUNKS - 2) as t:
                    chunk(g0 + t, True, True, False)
                chunk(g0 + CHUNKS - 2, True, False, False)
                chunk(g0 + CHUNKS - 1, False, False, not last)
                if not last:
                    first_scores(g0 + CHUNKS)

            for t in range(CHUNKS):
                renew_step(t, t)
                if t:
                    second_weights(t - 1)
            renew_step(CHUNKS, CHUNKS)
            first_scores(0)
            with dve.Fori(0, B - 1) as b:
                image(b, False)
            image(B - 1, True)


_INS = ["x", "L0_conv_wq", "L0_conv_bq", "L0_conv_wk", "L0_conv_bk", "L0_conv_wv", "L0_conv_bv",
        "L0_conv_wo", "L0_conv_bo", "L1_conv_wc"]


def kernel(**inputs):
    import numpy as _np
    import concourse.bacc as _bacc
    from concourse import mybir as _mybir
    from concourse.bass_utils import run_bass_kernel_spmd as _run

    nc = _bacc.Bacc("TRN2", target_bir_lowering=False, num_devices=1)
    arrays, args = {}, []
    for name in _INS:
        a = _np.ascontiguousarray(inputs[name])
        arrays[f"in_{name}_dram"] = a
        args.append(nc.dram_tensor(f"in_{name}_dram", a.shape, _mybir.dt.from_np(a.dtype),
                                   kind="ExternalInput").ap())
    shape = tuple(inputs["x"].shape)
    out = nc.dram_tensor("out_dram", shape, _mybir.dt.float32, kind="ExternalOutput").ap()
    attention_conv_kernel(nc, *args, out)
    r = _run(nc, [arrays], core_ids=[0])
    return r.results[0]["out_dram"]
```
